# Optimizing a Trainium2 kernel written in Bass

```python
import numpy as np
import jax
import jax.numpy as jnp

def _softmax(x, axis=-1):
    return jax.nn.softmax(x, axis=axis)
def _gelu(x):
    return jax.nn.gelu(x, approximate=True)
def _silu(x):
    return jax.nn.silu(x)
def _sigmoid(x):
    return jax.nn.sigmoid(x)
def _layernorm(x, axis=-1, eps=1e-5):
    m = jnp.mean(x, axis=axis, keepdims=True)
    v = jnp.var(x, axis=axis, keepdims=True)
    return (x - m) / jnp.sqrt(v + eps)
def _scatter_add(tgt, idx, src, axis=0):
    return tgt.at[idx].add(src)
def _segment_sum(src, seg, n):
    return jax.ops.segment_sum(src, seg, n)

kernel_name = 'mk_conv_seq_d2_conv_nchw64_24d90a'

def setup_inputs(seed: int = 0):
    np.random.seed(seed)
    _w = jnp.asarray
    def _rec_inputs():
        import jax
        import jax.numpy as jnp
        _gk = jax.random.key(seed)
        x = -0.000125 + 0.9999 * jax.random.normal(jax.random.fold_in(_gk, 1), (8, 64, 256, 256), jnp.float32)
        return x
    x = _rec_inputs()
    def _L0_conv_setup():
        import jax, jax.numpy as jnp
        import numpy as np
        C = 64
        WS = 8
        SCALE = 1.0 / C ** 0.5

        def conv1x1(x, w, b):
            return jnp.einsum('bchw,oc->bohw', x, w) + b[None, :, None, None]

        def to_windows(t):
            B, c, H, W = t.shape
            t = t.reshape(B, c, H // WS, WS, W // WS, WS)
            t = t.transpose(0, 2, 4, 3, 5, 1)
            return t.reshape(-1, WS * WS, c)

        def from_windows(t, B, H, W):
            c = t.shape[-1]
            t = t.reshape(B, H // WS, W // WS, WS, WS, c)
            t = t.transpose(0, 5, 1, 3, 2, 4)
            return t.reshape(B, c, H, W)
        key = jax.random.key(seed)
        ks = jax.random.split(key, 24)
        s = 0.02
        d = {'x': jax.random.normal(ks[0], (8, C, 256, 256), jnp.float32), 'qk_w': jax.random.normal(ks[1], (2 * C, C), jnp.float32) * s, 'qk_b': jnp.zeros((2 * C,), jnp.float32), 'v_w': jax.random.normal(ks[2], (C, C), jnp.float32) * s, 'v_b': jnp.zeros((C,), jnp.float32), 'out_w': jax.random.normal(ks[3], (C, C), jnp.float32) * s, 'out_b': jnp.zeros((C,), jnp.float32), 'ms1_w': jax.random.normal(ks[4], (C // 2, C, 3, 3), jnp.float32) * s, 'ms1_b': jnp.zeros((C // 2,), jnp.float32), 'ms2_w': jax.random.normal(ks[5], (C, C // 2), jnp.float32) * s, 'ms2_b': jnp.zeros((C,), jnp.float32), 'se1_w': jax.random.normal(ks[6], (C // 16, C), jnp.float32) * s, 'se1_b': jnp.zeros((C // 16,), jnp.float32), 'se2_w': jax.random.normal(ks[7], (C, C // 16), jnp.float32) * s, 'se2_b': jnp.zeros((C,), jnp.float32), 'ln_g': jnp.ones((C,), jnp.float32), 'ln_b': jnp.zeros((C,), jnp.float32), 'fc1_w': jax.random.normal(ks[8], (C, C), jnp.float32) * s, 'fc1_b': jnp.zeros((C,), jnp.float32), 'fc2_w': jax.random.normal(ks[9], (C, C), jnp.float32) * s, 'fc2_b': jnp.zeros((C,), jnp.float32)}
        return d
    _L0_conv_all = _L0_conv_setup()
    _L0_conv_in = {k: v for k, v in _L0_conv_all.items() if k in ('qk_w', 'qk_b', 'v_w', 'v_b', 'out_w', 'out_b', 'ms1_w', 'ms1_b', 'ms2_w', 'ms2_b', 'se1_w', 'se1_b', 'se2_w', 'se2_b', 'ln_g', 'ln_b', 'fc1_w', 'fc1_b', 'fc2_w', 'fc2_b', )}
    del _L0_conv_all

    def _L1_conv_setup():
        import jax, jax.numpy as jnp
        import numpy as np
        from jax import lax
        CUTOFF = 0.25
        SIGMA = 1.0
        RADIUS = 4

        def _gauss_kernel(sigma=SIGMA, radius=RADIUS):
            x = np.arange(-radius, radius + 1, dtype=np.float32)
            k = np.exp(-0.5 * (x / sigma) ** 2)
            return jnp.asarray(k / k.sum())

        def _blur_axis(x, axis, kernel):
            r = (kernel.shape[0] - 1) // 2
            pad = [(0, 0)] * x.ndim
            pad[axis] = (r, r)
            xp = jnp.pad(x, pad, mode='edge')
            out = jnp.zeros_like(x)
            for i in range(kernel.shape[0]):
                out = out + kernel[i] * lax.slice_in_dim(xp, i, i + x.shape[axis], axis=axis)
            return out

        def gaussian_smoothing_4d(x):
            k = _gauss_kernel().astype(x.dtype)
            for ax in range(4):
                x = _blur_axis(x, ax, k)
            return x

        def dht_2d(x):
            return (jnp.fft.fftn(x, axes=(2, 3)).real - jnp.fft.fftn(jnp.flip(x, axis=(2, 3)), axes=(2, 3)).imag).astype(x.dtype)

        def _neg_k(a):
            return jnp.roll(jnp.flip(a, axis=(-2, -1)), shift=(1, 1), axis=(-2, -1))

        def compl_mul2d(x1, x2):
            x1n, x2n = (_neg_k(x1), _neg_k(x2))
            e = lambda a, b: jnp.einsum('bixy,ioxy->boxy', a, b)
            return 0.5 * (e(x1, x2) - e(x1n, x2n) + e(x1, x2n) + e(x1n, x2))
        key = jax.random.key(seed)
        k1, k2 = jax.random.split(key)
        B, Cin, Cout, H, W, M1, M2 = (16, 64, 64, 128, 128, 20, 20)
        x = jax.random.normal(k1, (B, Cin, H, W), dtype=jnp.float32)
        scale = 1.0 / (Cin * Cout)
        w1 = scale * jax.random.uniform(k2, (Cin, Cout, M1, M2), dtype=jnp.float32)
        return {'x': x, 'w1': w1}
    _L1_conv_all = _L1_conv_setup()
    _L1_conv_in = {k: v for k, v in _L1_conv_all.items() if k in ('w1', )}
    del _L1_conv_all

    return {
        "x": x,
        "L0_conv_qk_w": _L0_conv_in["qk_w"],
        "L0_conv_qk_b": _L0_conv_in["qk_b"],
        "L0_conv_v_w": _L0_conv_in["v_w"],
        "L0_conv_v_b": _L0_conv_in["v_b"],
        "L0_conv_out_w": _L0_conv_in["out_w"],
        "L0_conv_out_b": _L0_conv_in["out_b"],
        "L0_conv_ms1_w": _L0_conv_in["ms1_w"],
        "L0_conv_ms1_b": _L0_conv_in["ms1_b"],
        "L0_conv_ms2_w": _L0_conv_in["ms2_w"],
        "L0_conv_ms2_b": _L0_conv_in["ms2_b"],
        "L0_conv_se1_w": _L0_conv_in["se1_w"],
        "L0_conv_se1_b": _L0_conv_in["se1_b"],
        "L0_conv_se2_w": _L0_conv_in["se2_w"],
        "L0_conv_se2_b": _L0_conv_in["se2_b"],
        "L0_conv_ln_g": _L0_conv_in["ln_g"],
        "L0_conv_ln_b": _L0_conv_in["ln_b"],
        "L0_conv_fc1_w": _L0_conv_in["fc1_w"],
        "L0_conv_fc1_b": _L0_conv_in["fc1_b"],
        "L0_conv_fc2_w": _L0_conv_in["fc2_w"],
        "L0_conv_fc2_b": _L0_conv_in["fc2_b"],
        "L1_conv_w1": _L1_conv_in["w1"],
    }

def reference(x, L0_conv_qk_w, L0_conv_qk_b, L0_conv_v_w, L0_conv_v_b, L0_conv_out_w, L0_conv_out_b, L0_conv_ms1_w, L0_conv_ms1_b, L0_conv_ms2_w, L0_conv_ms2_b, L0_conv_se1_w, L0_conv_se1_b, L0_conv_se2_w, L0_conv_se2_b, L0_conv_ln_g, L0_conv_ln_b, L0_conv_fc1_w, L0_conv_fc1_b, L0_conv_fc2_w, L0_conv_fc2_b, L1_conv_w1):
    import jax
    import jax.numpy as jnp
    def _L0_conv_ref(x, qk_w, qk_b, v_w, v_b, out_w, out_b, ms1_w, ms1_b, ms2_w, ms2_b, se1_w, se1_b, se2_w, se2_b, ln_g, ln_b, fc1_w, fc1_b, fc2_w, fc2_b):
        import jax, jax.numpy as jnp
        import numpy as np
        C = 64
        WS = 8
        SCALE = 1.0 / C ** 0.5

        def conv1x1(x, w, b):
            return jnp.einsum('bchw,oc->bohw', x, w) + b[None, :, None, None]

        def to_windows(t):
            B, c, H, W = t.shape
            t = t.reshape(B, c, H // WS, WS, W // WS, WS)
            t = t.transpose(0, 2, 4, 3, 5, 1)
            return t.reshape(-1, WS * WS, c)

        def from_windows(t, B, H, W):
            c = t.shape[-1]
            t = t.reshape(B, H // WS, W // WS, WS, WS, c)
            t = t.transpose(0, 5, 1, 3, 2, 4)
            return t.reshape(B, c, H, W)
        B, c, H, W = x.shape
        qk = conv1x1(x, qk_w, qk_b)
        q, k = jnp.split(qk, 2, axis=1)
        v = conv1x1(x, v_w, v_b)
        qw, kw, vw = (to_windows(q), to_windows(k), to_windows(v))
        attn = jnp.einsum('ntc,nsc->nts', qw, kw) * SCALE
        attn = jax.nn.softmax(attn, axis=-1)
        ow = jnp.einsum('nts,nsc->ntc', attn, vw)
        attn_out = conv1x1(from_windows(ow, B, H, W), out_w, out_b)
        gap = x.mean(axis=(2, 3))
        se = jax.nn.relu(gap @ se1_w.T + se1_b)
        gate = jax.nn.sigmoid(se @ se2_w.T + se2_b)
        attn_out = attn_out * gate[:, :, None, None]
        ms = jax.lax.conv_general_dilated(x, ms1_w, (1, 1), 'SAME', dimension_numbers=('NCHW', 'OIHW', 'NCHW'))
        ms = jax.nn.relu(ms + ms1_b[None, :, None, None])
        ms = conv1x1(ms, ms2_w, ms2_b)
        x1 = x + attn_out + ms
        t = x1.transpose(0, 2, 3, 1)
        mu = t.mean(-1, keepdims=True)
        var = ((t - mu) ** 2).mean(-1, keepdims=True)
        tn = (t - mu) * jax.lax.rsqrt(var + 1e-05) * ln_g + ln_b
        h = jax.nn.gelu(tn @ fc1_w.T + fc1_b)
        ffn = h @ fc2_w.T + fc2_b
        out = x1 + ffn.transpose(0, 3, 1, 2)
        return out

    def _L1_conv_ref(x, w1):
        import jax, jax.numpy as jnp
        import numpy as np
        from jax import lax
        CUTOFF = 0.25
        SIGMA = 1.0
        RADIUS = 4

        def _gauss_kernel(sigma=SIGMA, radius=RADIUS):
            x = np.arange(-radius, radius + 1, dtype=np.float32)
            k = np.exp(-0.5 * (x / sigma) ** 2)
            return jnp.asarray(k / k.sum())

        def _blur_axis(x, axis, kernel):
            r = (kernel.shape[0] - 1) // 2
            pad = [(0, 0)] * x.ndim
            pad[axis] = (r, r)
            xp = jnp.pad(x, pad, mode='edge')
            out = jnp.zeros_like(x)
            for i in range(kernel.shape[0]):
                out = out + kernel[i] * lax.slice_in_dim(xp, i, i + x.shape[axis], axis=axis)
            return out

        def gaussian_smoothing_4d(x):
            k = _gauss_kernel().astype(x.dtype)
            for ax in range(4):
                x = _blur_axis(x, ax, k)
            return x

        def dht_2d(x):
            return (jnp.fft.fftn(x, axes=(2, 3)).real - jnp.fft.fftn(jnp.flip(x, axis=(2, 3)), axes=(2, 3)).imag).astype(x.dtype)

        def _neg_k(a):
            return jnp.roll(jnp.flip(a, axis=(-2, -1)), shift=(1, 1), axis=(-2, -1))

        def compl_mul2d(x1, x2):
            x1n, x2n = (_neg_k(x1), _neg_k(x2))
            e = lambda a, b: jnp.einsum('bixy,ioxy->boxy', a, b)
            return 0.5 * (e(x1, x2) - e(x1n, x2n) + e(x1, x2n) + e(x1n, x2))
        B, _, H, W = x.shape
        Cout, M1, M2 = (w1.shape[1], w1.shape[2], w1.shape[3])
        x_ht = dht_2d(x)
        out_ht = jnp.zeros((B, Cout, H, W), dtype=x.dtype)
        out_ht = out_ht.at[:, :, :M1, :M2].set(compl_mul2d(x_ht[:, :, :M1, :M2], w1))
        y = dht_2d(out_ht) / (H * W)
        y = gaussian_smoothing_4d(y)
        freqs = jnp.fft.fftfreq(W)
        mask = (jnp.abs(freqs) <= CUTOFF).astype(y.dtype)
        return y * mask

    def _gn(v, G=32, eps=1e-5):
        B_, C_, H_, W_ = v.shape
        g = v.reshape(B_, G, C_ // G, H_, W_)
        m = jnp.mean(g, axis=(2, 3, 4), keepdims=True)
        s = jnp.var(g, axis=(2, 3, 4), keepdims=True)
        return ((g - m) / jnp.sqrt(s + eps)).reshape(v.shape)

    def _ln_c(v, eps=1e-6):
        m = jnp.mean(v, axis=1, keepdims=True)
        s = jnp.var(v, axis=1, keepdims=True)
        return (v - m) / jnp.sqrt(s + eps)

    def _ln_t(v, eps=1e-5):
        m = jnp.mean(v, axis=-1, keepdims=True)
        s = jnp.var(v, axis=-1, keepdims=True)
        return (v - m) / jnp.sqrt(s + eps)

    def _to_tokens(v):
        B_, C_, H_, W_ = v.shape
        return v.reshape(B_, C_, H_ * W_).transpose(0, 2, 1)
    def _from_tokens(t, like):
        B_, C_, H_, W_ = like.shape
        return t.transpose(0, 2, 1).reshape(B_, C_, H_, W_)

    x = _L0_conv_ref(x, L0_conv_qk_w, L0_conv_qk_b, L0_conv_v_w, L0_conv_v_b, L0_conv_out_w, L0_conv_out_b, L0_conv_ms1_w, L0_conv_ms1_b, L0_conv_ms2_w, L0_conv_ms2_b, L0_conv_se1_w, L0_conv_se1_b, L0_conv_se2_w, L0_conv_se2_b, L0_conv_ln_g, L0_conv_ln_b, L0_conv_fc1_w, L0_conv_fc1_b, L0_conv_fc2_w, L0_conv_fc2_b)
    x = _L1_conv_ref(x, L1_conv_w1)
    return x


_drawn_inputs = setup_inputs


def setup_inputs(seed=0):
    import zlib

    import numpy as np

    out = dict(_drawn_inputs(seed))
    spreads = {'L0_conv_qk_b': (0.0, 0.8),
     'L0_conv_v_b': (0.0, 0.1),
     'L0_conv_out_b': (0.0, 0.1),
     'L0_conv_ms1_b': (0.0, 0.1),
     'L0_conv_ms2_b': (0.0, 0.1),
     'L0_conv_se1_b': (0.0, 0.8),
     'L0_conv_se2_b': (0.0, 0.8),
     'L0_conv_ln_g': (1.0, 0.6),
     'L0_conv_ln_b': (0.0, 2.0),
     'L0_conv_fc1_b': (0.0, 0.283),
     'L0_conv_fc2_b': (0.0, 0.1)}
    factors = {'L0_conv_qk_w': 8.0,
     'L0_conv_v_w': 8.0,
     'L0_conv_out_w': 2.678,
     'L0_conv_ms1_w': 5.552,
     'L0_conv_se1_w': 64.0,
     'L0_conv_se2_w': 8.0}
    for name, (base, spread) in spreads.items():
        noise = np.random.default_rng([zlib.crc32(name.encode()), seed]).standard_normal(out[name].shape)
        drawn = base * np.exp(spread * noise) if base else spread * noise
        out[name] = jnp.asarray(drawn.astype(out[name].dtype))
    for name, factor in factors.items():
        out[name] = (out[name] * factor).astype(out[name].dtype)
    return out
```

```python
from contextlib import ExitStack

import numpy as np
import concourse.bass as bass
from concourse import mybir

F32 = mybir.dt.float32
ALU = mybir.AluOpType
ACT = mybir.ActivationFunctionType
AX_X = mybir.AxisListType.X

B, C, H, W = 8, 64, 256, 256
PAIRS = B // 2
WS = 8
STRIPS = H // WS
WIN = W // WS
HALF = W // 2
PX = WS * W
HID = C // 2
SE = C // 16
M = 20
MM = M * M
COMP = 2 * M
M1 = M + 1
KEPT_LO, KEPT_HI = 65, 64
KEPT = KEPT_LO + KEPT_HI
SCALE = 1.0 / C ** 0.5
LN_EPS = 1e-5
CH = 4
BANK = 512


def blur_matrix(n, sigma=1.0, radius=4):
    t = np.arange(-radius, radius + 1, dtype=np.float32)
    k = np.exp(-0.5 * (t / sigma) ** 2)
    k = (k / k.sum()).astype(np.float64)
    g = np.zeros((n, n))
    for i in range(n):
        for j in range(2 * radius + 1):
            g[i, min(max(i + j - radius, 0), n - 1)] += k[j]
    return g


def shape_constants():
    two_pi = 2 * np.pi
    ident = np.eye(128)
    ang = two_pi * np.outer(np.arange(W), np.arange(M)) / W
    colb = np.concatenate([np.cos(ang), np.sin(ang)], 1).reshape(2, 128, COMP).transpose(1, 0, 2)
    h = np.arange(H)[:, None, None]
    k2 = np.arange(M)[None, :, None]
    k1 = np.arange(M)[None, None, :]
    a1 = two_pi * h * k1 / H
    phi = two_pi * (k1 + k2) / H
    rowb = np.stack([np.cos(a1) - np.sin(a1 + phi), -np.sin(a1) - np.cos(a1 + phi)], 2)
    rowb = rowb.reshape(2, 128, M, 2, M).transpose(1, 0, 2, 3, 4)
    m = np.arange(M1)
    inv = np.zeros((2, 32, H))
    inv[0, :M1] = np.cos(two_pi * np.outer(m, np.arange(H)) / H)
    inv[1, :M1] = np.sin(two_pi * np.outer(m, np.arange(H)) / H)
    inv = (inv.reshape(64, H) @ blur_matrix(H).T) * (0.5 / (H * W))
    inv = np.concatenate([inv, inv], 0)
    keep = np.r_[0:KEPT_LO, W - KEPT_HI:W]
    c = np.cos(two_pi * np.outer(m, np.arange(W)) / W)
    s = np.sin(two_pi * np.outer(m, np.arange(W)) / W)
    invc = np.zeros((64, 2, W))
    invc[0:M1, 0], invc[32:32 + M1, 0], invc[0:M1, 1], invc[32:32 + M1, 1] = c, -s, -s, -c
    invc = (invc @ blur_matrix(W).T)[:, :, keep]
    center = np.eye(C) - 1.0 / C
    return {
        "k_ident": ident, "k_colb": colb, "k_rowb": rowb.reshape(128, -1), "k_inv": inv,
        "k_invc": invc, "k_center": np.concatenate([center, center], 1), "k_blurc": blur_matrix(C).T,
    }


def conv_layer_then_hartley_kernel(nc, t, out):
    x_pair = t["x"].rearrange("(p a) c h w -> p (a c) h w", a=2)
    blur_b = blur_matrix(B)
    comps = nc.dram_tensor("mode_columns", [PAIRS, H, COMP, 2, 2 * C], F32, kind="Internal").ap()

    top = ExitStack()
    with top:
        def keep_sb(name, shape):
            return top.enter_context(nc.sbuf_tensor(name, shape, F32))

        ident = keep_sb("ident", [128, 128])
        g_w = keep_sb("g_w", [128, 128])
        g_b = keep_sb("g_b", [128, 1])
        val_w_all = keep_sb("val_w_all", [128, PAIRS, 128])
        val_b_all = keep_sb("val_b_all", [128, PAIRS, 128])
        conv_w = keep_sb("conv_w", [128, 12, 128])
        conv_b = keep_sb("conv_b", [128, 1])
        ms2_w = keep_sb("ms2_w", [128, 2, 128])
        ffn_w = keep_sb("ffn_w", [128, 256])
        ffn_b = keep_sb("ffn_b", [128, 128])
        fc2_w = keep_sb("fc2_w", [128, 2, 128])
        same_w = keep_sb("same_w", [128, 2, 128])
        fc2_b = keep_sb("fc2_b", [128, 1])

        prepare(nc, t, x_pair, locals())
        main(nc, t, x_pair, comps, locals())
        modes_and_output(nc, t, comps, out, blur_b, locals())


def prepare(nc, t, x_pair, keep):
    with ExitStack() as ctx:
        def sb(name, shape):
            return ctx.enter_context(nc.sbuf_tensor(name, shape, F32))

        def sem(name):
            return ctx.enter_context(nc.semaphore(name))

        ident, g_w, g_b = keep["ident"], keep["g_w"], keep["g_b"]
        val_w_all, val_b_all = keep["val_w_all"], keep["val_b_all"]
        conv_w, conv_b, ms2_w = keep["conv_w"], keep["conv_b"], keep["ms2_w"]
        ffn_w, ffn_b, fc2_w, same_w, fc2_b = (keep[k] for k in ("ffn_w", "ffn_b", "fc2_w", "same_w", "fc2_b"))

        PIECE = 32
        PIECES = H // PIECE
        xs = sb("xs", [128, 2, PIECE * W])
        junk = sb("junk", [128, PIECE * W])
        sums = sb("sums", [128, PAIRS, PIECES])
        gap = sb("gap", [128, PAIRS])
        wq2 = sb("wq2", [C, 2, C])
        wk2 = sb("wk2", [C, 2, C])
        bq = sb("bq", [C, 1])
        vw2 = sb("vw2", [C, 2, C])
        vb = sb("vb", [C, 1])
        ow_t = sb("ow_t", [C, C])
        ob = sb("ob", [C, 1])
        ms1_raw = sb("ms1_raw", [HID, C * 9])
        conv_t = sb("conv_t", [128, 9, HID])
        ms2b_row = sb("ms2b_row", [128, C])
        se1_t = sb("se1_t", [128, SE])
        se1_b = sb("se1_b", [SE, 1])
        se2_t = sb("se2_t", [SE, 2, C])
        se2_b = sb("se2_b", [128, 1])
        fc1_t = sb("fc1_t", [C, C])
        ln_g = sb("ln_g", [C, 1])
        ln_b = sb("ln_b", [C, 1])
        fc1b_row = sb("fc1b_row", [128, C])
        fc2b_raw = sb("fc2b_raw", [128, 1])
        center = sb("center", [C, 128])
        fc1_g = sb("fc1_g", [C, C])
        ln_b_wide = sb("ln_b_wide", [C, 128])
        hidden = sb("hidden", [SE, 2, PAIRS])
        gate = sb("gate", [128, 2, PAIRS])
        gate_wide = sb("gate_wide", [C, 2 * PAIRS, 128])
        gate_row = sb("gate_row", [128, 2, PAIRS, C])
        obv = sb("obv", [C, 1])
        obv_wide = sb("obv_wide", [C, 128])
        obv_row = sb("obv_row", [128, C])
        vw_plain = sb("vw_plain", [128, C])
        pA = ctx.enter_context(nc.psum_tensor("pA", [128, BANK], F32))
        pB = ctx.enter_context(nc.psum_tensor("pB", [128, BANK], F32))
        pC = ctx.enter_context(nc.psum_tensor("pC", [128, BANK], F32))
        pD = ctx.enter_context(nc.psum_tensor("pD", [128, BANK], F32))

        weights_in, zeroed, placed = sem("weights_in"), sem("zeroed"), sem("placed")
        piece_in = [sem("piece_in0"), sem("piece_in1")]
        piece_sum = sem("piece_sum")
        dve, pe, act = sem("dve_step"), sem("pe_step"), sem("act_step")

        def vec(name):
            return t[name].rearrange("(c o) -> c o", o=1)

        loads = [
            (ident[:], t["k_ident"]), (center[:], t["k_center"]),
            (bq[:], vec("qk_b")[0:C]), (vb[:], vec("v_b")), (ob[:], vec("out_b")),
            (ms1_raw[:], t["ms1_w"].rearrange("o c kh kw -> o (c kh kw)")),
            (ms2b_row[:], t["ms2_b"].partition_broadcast(128)),
            (fc1b_row[:], t["fc1_b"].partition_broadcast(128)),
            (se1_b[:], vec("se1_b")), (ln_g[:], vec("ln_g")), (ln_b[:], vec("ln_b")),
            (fc1_t[:], t["fc1_w"].rearrange("o c -> c o")),
            (ow_t[:], t["out_w"].rearrange("o c -> c o")),
        ]
        for a in range(2):
            lo, hi = a * C, a * C + C
            loads += [
                (wq2[:, a, :], t["qk_w"][0:C, :]), (wk2[:, a, :], t["qk_w"][C:2 * C, :]),
                (vw2[:, a, :], t["v_w"]), (se2_b[lo:hi, :], vec("se2_b")),
                (se1_t[lo:hi, :], t["se1_w"].rearrange("o c -> c o")),
                (se2_t[:, a, :], t["se2_w"].rearrange("o c -> c o")),
                (fc2b_raw[lo:hi, :], vec("fc2_b")),
            ]
            for par in range(2):
                r = par * C + a * HID
                loads += [(conv_b[r:r + HID, :], vec("ms1_b"))]
        late = []
        for a in range(2):
            for par in range(2):
                r = par * C + a * HID
                late += [(ms2_w[r:r + HID, par, a * C:a * C + C], t["ms2_w"].rearrange("o c -> c o"))]
                late += [(fc2_w[a * C:a * C + C, a, par * C:par * C + C], t["fc2_w"].rearrange("o c -> c o")),
                         (same_w[a * C:a * C + C, a, par * C:par * C + C], t["k_ident"][0:C, 0:C])]

        block = ctx.enter_context(nc.Block())

        @block.sync
        def _(sp):
            for q in range(PAIRS * PIECES):
                if q >= 2:
                    sp.wait_ge(piece_sum, q - 1)
                sp.dma_start(xs[:, q % 2, :], x_pair[q // PIECES, :, (q % PIECES) * PIECE:(q % PIECES + 1) * PIECE, :]
                             .rearrange("c h w -> c (h w)")).then_inc(piece_in[q % 2], 16)

        @block.gpsimd
        def _(pool):
            for dst, src in loads:
                pool.dma_start(dst, src, allow_slow_non_contiguous=True).then_inc(weights_in, 16)
            pool.wait_ge(zeroed, 1)
            for dst, src in late:
                pool.dma_start(dst, src, allow_slow_non_contiguous=True).then_inc(placed, 16)
            pool.wait_ge(placed, 16 * len(late))

        @block.scalar
        def _(sc):
            for q in range(PAIRS * PIECES):
                sc.wait_ge(piece_in[q % 2], 16 * (q // 2 + 1))
                if q >= 1:
                    sc.wait_ge(piece_sum, q)
                sc.activation(junk[:], xs[:, q % 2, :], ACT.Copy,
                              accum_out=sums[:, q // PIECES, q % PIECES:q % PIECES + 1]).then_inc(piece_sum, 1)
            sc.wait_ge(pe, 5)
            sc.activation(hidden[:, 0, :], pC[0:SE, 0:PAIRS], ACT.Relu, bias=se1_b[:], scale=1.0 / (H * W))
            sc.activation(hidden[:, 1, :], pB[0:SE, 0:PAIRS], ACT.Relu, bias=se1_b[:], scale=1.0 / (H * W))\
                .then_inc(act, 1)
            sc.wait_ge(pe, 6)
            sc.activation(gate[:], pC[:, 16:16 + 2 * PAIRS].rearrange("c (a p) -> c a p", a=2), ACT.Sigmoid,
                          bias=se2_b[:]).then_inc(act, 1)

        @block.vector
        def _(v):
            steps = [0]

            def link(ins):
                steps[0] += 1
                ins.then_inc(dve, 1)
                v.wait_ge(dve, steps[0])

            for tile in (conv_w, ms2_w, fc2_w, same_w, ffn_w, g_w):
                v.memset(tile[:], 0.0)
            v.memset(val_w_all[:], 0.0).then_inc(zeroed, 1)
            v.wait_ge(zeroed, 1)
            v.wait_ge(weights_in, 16 * len(loads))
            link(v.tensor_scalar(fc1_g[:], fc1_t[:], ln_g[:], None, ALU.mult))
            link(v.tensor_copy(ln_b_wide[:], ln_b[:].to_broadcast([C, 128])))
            v.wait_ge(pe, 1)
            for a in range(2):
                s = slice(a * C, a * C + C)
                v.tensor_scalar(g_w[s, s], pA[s, 0:C], SCALE, None, ALU.mult)
            v.tensor_scalar(g_b[:], pA[:, 2 * C:2 * C + 1], SCALE, None, ALU.mult)
            v.tensor_scalar(fc2_b[:], fc2b_raw[:], float(H * W), None, ALU.mult)
            v.wait_ge(pe, 2)
            link(v.tensor_copy(conv_t[:], pB[:, 0:9 * HID].rearrange("c (k o) -> c k o", k=9)))
            for a in range(2):
                s = slice(a * C, a * C + C)
                for par in range(2):
                    for r in range(4):
                        kh = r - par
                        if 0 <= kh < 3:
                            o = par * C + a * HID
                            v.tensor_copy(conv_w[s, 3 * r:3 * r + 3, o:o + HID], conv_t[s, 3 * kh:3 * kh + 3, :])
            v.wait_ge(pe, 3)
            v.tensor_copy(ffn_w[:, 0:128], ident[:])
            for a in range(2):
                s = slice(a * C, a * C + C)
                v.tensor_copy(ffn_w[s, 128 + a * C:128 + a * C + C], pD[s, 0:C])
                v.tensor_tensor(ffn_b[:, s], pD[:, C:2 * C], fc1b_row[:], ALU.add)
            v.tensor_copy(vw_plain[:], pD[:, 2 * C:3 * C])
            link(v.tensor_tensor(obv[:], pD[0:C, 3 * C:3 * C + 1], ob[:], ALU.add))
            link(v.tensor_copy(obv_wide[:], obv[:].to_broadcast([C, 128])))
            v.wait_ge(pe, 4)
            link(v.tensor_copy(obv_row[:], pD[:, 256:256 + C]))
            v.wait_ge(piece_sum, PAIRS * PIECES)
            link(v.tensor_reduce(gap[:], sums[:], AX_X, ALU.add))
            v.wait_ge(act, 2)
            link(v.tensor_copy(gate_wide[:], gate[0:C].rearrange("c a p -> c (a p)").unsqueeze(2)
                               .to_broadcast([C, 2 * PAIRS, 128])))
            v.wait_ge(pe, 7)
            link(v.tensor_copy(gate_row[:], pA[:, 0:2 * PAIRS * C].rearrange("q (a p c) -> q a p c", a=2, p=PAIRS)))
            for a in range(2):
                s = slice(a * C, a * C + C)
                v.tensor_tensor(val_w_all[s, :, s], gate_row[s, a], vw_plain[s, :].unsqueeze(1)
                                .to_broadcast([C, PAIRS, C]), ALU.mult)
                link(v.tensor_tensor(val_b_all[:, :, s], gate_row[:, a], obv_row[:].unsqueeze(1)
                                     .to_broadcast([128, PAIRS, C]), ALU.mult))
                link(v.tensor_tensor(val_b_all[:, :, s], val_b_all[:, :, s], ms2b_row[:].unsqueeze(1)
                                     .to_broadcast([128, PAIRS, C]), ALU.add))

        @block.tensor
        def _(p):
            def mm(o, l, r, last=False):
                i = p.matmul(o, l, r, start=True, stop=True)
                if last:
                    i.then_inc(pe, 1)

            p.wait_ge(weights_in, 16 * len(loads))
            mm(pA[:, 0:C], wq2[:].rearrange("o a c -> o (a c)"), wk2[:, 0, :])
            mm(pA[:, 2 * C:2 * C + 1], wk2[:].rearrange("o a c -> o (a c)"), bq[:], True)
            raw = ms1_raw[:].rearrange("o (c k) -> o k c", k=9)
            for k in range(9):
                for a in range(2):
                    mm(pB[a * C:a * C + C, k * HID:k * HID + HID], raw[:, k, :], ident[0:HID, 0:HID], k == 8 and a == 1)
            p.wait_ge(dve, 2)
            mm(pD[:, 0:C], center[:], fc1_g[:])
            mm(pD[:, C:2 * C], ln_b_wide[:], fc1_t[:])
            mm(pD[:, 2 * C:3 * C], vw2[:].rearrange("o a c -> o (a c)"), ow_t[:])
            mm(pD[0:C, 3 * C:3 * C + 1], ow_t[:], vb[:], True)
            p.wait_ge(dve, 5)
            mm(pD[:, 256:256 + C], obv_wide[:], ident[0:C, 0:C], True)
            p.wait_ge(dve, 7)
            for a in range(2):
                s = slice(a * C, a * C + C)
                mm((pC, pB)[a][0:SE, 0:PAIRS], se1_t[s, :], gap[s, :], a == 1)
            p.wait_ge(act, 1)
            mm(pC[:, 16:16 + 2 * PAIRS], se2_t[:].rearrange("o a c -> o (a c)"),
               hidden[:].rearrange("c a p -> c (a p)"), True)
            p.wait_ge(dve, 8)
            for i in range(2 * PAIRS):
                mm(pA[:, i * C:i * C + C], gate_wide[:, i, :], ident[0:C, 0:C], i == 2 * PAIRS - 1)


def main(nc, t, x_pair, comps, keep):
    with ExitStack() as ctx:
        def sb(name, shape):
            return ctx.enter_context(nc.sbuf_tensor(name, shape, F32))

        def ps(name):
            return ctx.enter_context(nc.psum_tensor(name, [128, BANK], F32))

        def sem(name):
            return ctx.enter_context(nc.semaphore(name))

        def sems(name, n):
            return [sem(f"{name}{i}") for i in range(n)]

        g_w, g_b, conv_w, conv_b, ms2_w = (keep[k] for k in ("g_w", "g_b", "conv_w", "conv_b", "ms2_w"))
        ffn_w, ffn_b, ident = keep["ffn_w"], keep["ffn_b"], keep["ident"]
        val_w_all, val_b_all = keep["val_w_all"], keep["val_b_all"]

        TILES = PX // 128
        xt = [sb(f"xt{i}", [128, WS + 2, W + 2]) for i in range(2)]
        zrow = sb("zrow", [128, W])
        val_w = sb("val_w", [128, 128])
        val_b = sb("val_b", [128, 128])
        g = sb("g", [128, WIN, WS * WS])
        xw = sb("xw", [128, WIN, WS * WS])
        val = sb("val", [128, CH, 4, 128])
        prob = sb("prob", [128, CH, 8, 64])
        probT = sb("probT", [128, CH, 4, 128])
        mx = sb("mx", [128, CH, 8])
        den = sb("den", [128, CH, 8])
        rden = sb("rden", [128, CH, 8])
        hid = sb("hid", [128, 2, 4, HALF])
        x1 = sb("x1", [128, WS, W])
        ff = sb("ff", [128, TILES, 256])
        act_h = sb("act_h", [128, TILES, 128])
        stats = sb("stats", [128, TILES, 2, 6])
        dmean = sb("dmean", [128, TILES, 2])
        msum = sb("msum", [128, TILES, 2])
        dsq = sb("dsq", [128, TILES, 2])
        vare = sb("vare", [128, TILES, 2])
        rstd = sb("rstd", [128, TILES, 2])
        minus_half = sb("minus_half", [128, TILES, 2])
        colb = sb("colb", [128, 2, COMP])
        zs = sb("zs", [128, 2, BANK])
        proj = [ps("proj0"), ps("proj1")]
        wide = [ps("wide0"), ps("wide1")]
        acc = [ps("acc0"), ps("acc1")]
        scr = [ps("scr0"), ps("scr1")]

        x_in = sems("x_in", 2)
        consts_in, pads = sem("consts_in"), sem("pads")
        waited = sem("waited")
        pair_w = sem("pair_w")
        xw_sb = sems("xw_sb", CH)
        g_ps, g_sb = sems("g_ps", CH), sems("g_sb", CH)
        v_ps, v_sb = sems("v_ps", CH), sems("v_sb", CH)
        c_ps, c_sb = sems("c_ps", 2), sems("c_sb", 2)
        s_ps, s_max, s_sub = sems("s_ps", CH), sems("s_max", CH), sems("s_sub", CH)
        s_exp, s_sum, s_rec, s_nrm = sems("s_exp", CH), sems("s_sum", CH), sems("s_rec", CH), sems("s_nrm", CH)
        t_ps, t_sb = sems("t_ps", CH), sems("t_sb", CH)
        a_ps, x1_sb = sems("a_ps", 2), sems("x1_sb", 2)
        f_ps, f_sb = sems("f_ps", TILES // 2), sems("f_sb", TILES // 2)
        stat_ok, dm_ok, q_ok, ve_ok, var_ok = sem("stat_ok"), sem("dm_ok"), sem("q_ok"), sem("ve_ok"), sem("var_ok")
        rstd_ok = sem("rstd_ok")
        hmul, hbias, hact = sem("hmul"), sem("hbias"), sem("hact")
        z_ps, z_sb = sems("z_ps", 2), sems("z_sb", 2)
        z_out = sem("z_out")

        zv = comps.rearrange("p (s r) k m c -> p s m k r c", r=WS)

        block = ctx.enter_context(nc.Block())

        @block.sync
        def _(sp):
            sp.dma_start(colb[:], t["k_colb"]).then_inc(consts_in, 16)
            sp.wait_ge(pads, 2)

            def load(pair, s, n1, par, first=False, last=False):
                tile = xt[par]
                sp.wait_ge(x1_sb[1], n1)
                r0 = s * WS
                if first:
                    sp.dma_start(tile[:, 0, 1:W + 1], zrow[:]).then_inc(x_in[par], 16)
                else:
                    sp.dma_start(tile[:, 0, 1:W + 1], x_pair[pair, :, bass.ds(r0 - 1, 1), :]
                                 .rearrange("c h w -> c (h w)")).then_inc(x_in[par], 16)
                sp.dma_start(tile[:, 1:WS + 1, 1:W + 1], x_pair[pair, :, bass.ds(r0, WS), :]).then_inc(x_in[par], 16)
                if last:
                    sp.dma_start(tile[:, WS + 1, 1:W + 1], zrow[:]).then_inc(x_in[par], 16)
                else:
                    sp.dma_start(tile[:, WS + 1, 1:W + 1], x_pair[pair, :, bass.ds(r0 + WS, 1), :]
                                 .rearrange("c h w -> c (h w)")).then_inc(x_in[par], 16)

            with sp.Fori(0, PAIRS) as pair:
                n0 = sp.snap(pair * STRIPS + 1)
                load(pair, 0, n0, 0, first=True)
                with sp.Fori(0, STRIPS // 2 - 1) as i:
                    for j in range(2):
                        s = sp.snap(i * 2 + (1 + j))
                        load(pair, s, sp.snap(n0 + s), (1 + j) % 2)
                load(pair, STRIPS - 1, sp.snap(n0 + (STRIPS - 1)), 1, last=True)

        @block.gpsimd
        def _(pool):
            pool.memset(minus_half[:], -0.5)

            def attention(n1):
                for j in range(CH):
                    pool.wait_ge(s_rec[j], n1)
                    pool.tensor_tensor(prob[:, j], prob[:, j], rden[:, j].unsqueeze(2).to_broadcast([128, 8, 64]),
                                       ALU.mult).then_inc(s_nrm[j], 1)

            def feed_forward(m1):
                pool.wait_ge(var_ok, m1)
                pool.tensor_tensor(rstd[:], vare[:], minus_half[:], ALU.pow).then_inc(rstd_ok, 1)
                pool.wait_ge(hmul, m1)
                pool.tensor_tensor(act_h[:], act_h[:], ffn_b[:].unsqueeze(1).to_broadcast([128, TILES, 128]),
                                   ALU.add).then_inc(hbias, 1)

            def strips(eng):
                with eng.Fori(0, PAIRS) as pair:
                    n0 = eng.snap(pair * STRIPS + 1)
                    attention(n0)
                    with eng.Fori(0, STRIPS // 2 - 1) as i:
                        for j in range(2):
                            n1 = eng.snap(n0 + i * 2 + (1 + j))
                            attention(n1)
                            feed_forward(eng.snap(n1 - 1))
                    last = eng.snap(n0 + (STRIPS - 1))
                    attention(last)
                    feed_forward(eng.snap(last - 1))
                    feed_forward(last)

            strips(pool)

        @block.scalar
        def _(sc):
            def attention(n1):
                relu(n1, 0)
                for j in range(CH):
                    sc.wait_ge(g_ps[j], n1)
                    sc.activation(g[:, 8 * j:8 * j + 8].rearrange("c k w -> c (k w)"), proj[j % 2][:],
                                  ACT.Identity, bias=g_b[:]).then_inc(g_sb[j], 1)
                for j in range(CH):
                    sc.wait_ge(s_sub[j], n1)
                    sc.activation(prob[:, j], prob[:, j], ACT.Exp).then_inc(s_exp[j], 1)
                relu(n1, 1)

            def relu(n1, q):
                sc.wait_ge(c_ps[q], n1)
                sc.activation(hid[:, q], wide[q][:].rearrange("c (r w) -> c r w", r=4), ACT.Relu,
                              bias=conv_b[:]).then_inc(c_sb[q], 1)

            def transposed(n1):
                for j in range(CH):
                    sc.wait_ge(t_ps[j], n1)
                    sc.activation(probT[:, j], proj[j % 2][:].rearrange("c (r w) -> c r w", r=4),
                                  ACT.Identity).then_inc(t_sb[j], 1)

            def token_major(m1):
                for k in range(TILES // 2):
                    sc.wait_ge(f_ps[k], m1)
                    sc.activation(ff[:, 2 * k:2 * k + 2, :], scr[k % 2][:].rearrange("c (r w) -> c r w", r=2),
                                  ACT.Identity).then_inc(f_sb[k], 1)

            def gelu(m1):
                sc.wait_ge(hbias, m1)
                sc.activation(act_h[:], act_h[:], ACT.Gelu_apprx_tanh).then_inc(hact, 1)

            def components(m1, m32):
                for r in range(2):
                    sc.wait_ge(z_ps[r], m1)
                    if r == 0:
                        sc.wait_ge(z_out, m32)
                    sc.activation(zs[0:COMP, r, :], wide[r][0:COMP, :], ACT.Identity)
                    sc.activation(zs[64:64 + COMP, r, :], wide[r][64:64 + COMP, :], ACT.Identity).then_inc(z_sb[r], 1)

            def store(pair, s, m1):
                sc.wait_ge(z_sb[0], m1 + 1)
                sc.wait_ge(z_sb[1], m1 + 1)
                for part in range(2):
                    sc.dma_start(zv[pair, s, part], zs[64 * part:64 * part + COMP].rearrange(
                        "k g (r c) -> k (g r) c", r=4)).then_inc(z_out, 16)

            def whole(pair, s, m1):
                gelu(m1)
                components(m1, sc.snap(m1 * 32))
                store(pair, s, m1)

            sc.sem_inc(z_out, 32)
            sc.sem_inc(z_sb[0], 1)
            sc.sem_inc(z_sb[1], 1)
            with sc.Fori(0, PAIRS) as pair:
                n0 = sc.snap(pair * STRIPS + 1)
                attention(n0)
                transposed(n0)
                with sc.Fori(0, STRIPS // 2 - 1) as i:
                    for j in range(2):
                        s = sc.snap(i * 2 + (1 + j))
                        n1 = sc.snap(n0 + s)
                        m1 = sc.snap(n1 - 1)
                        attention(n1)
                        token_major(m1)
                        transposed(n1)
                        whole(pair, sc.snap(s - 1), m1)
                last = sc.snap(n0 + (STRIPS - 1))
                before = sc.snap(last - 1)
                attention(last)
                token_major(before)
                transposed(last)
                whole(pair, STRIPS - 2, before)
                token_major(last)
                whole(pair, STRIPS - 1, last)
            sc.wait_ge(z_out, 32 * (PAIRS * STRIPS + 1))

        @block.vector
        def _(v):
            v.memset(zrow[:], 0.0).then_inc(pads, 1)
            v.memset(xt[0][:, :, 0:W + 2:W + 1], 0.0)
            v.memset(xt[1][:, :, 0:W + 2:W + 1], 0.0).then_inc(pads, 1)

            def values(n1):
                for j in range(CH):
                    v.wait_ge(v_ps[j], n1)
                    v.tensor_tensor(val[:, j], proj[j % 2][:].rearrange("c (r w) -> c r w", r=4),
                                    val_b[:].unsqueeze(1).to_broadcast([128, 4, 128]), ALU.add).then_inc(v_sb[j], 1)

            def softmax(n1):
                for j in range(CH):
                    scores = scr[j % 2][:].rearrange("c (r w) -> c r w", r=8)
                    v.wait_ge(s_ps[j], n1)
                    v.tensor_reduce(mx[:, j], scores, AX_X, ALU.max).then_inc(s_max[j], 1)
                    v.wait_ge(s_max[j], n1)
                    v.tensor_tensor(prob[:, j], scores, mx[:, j].unsqueeze(2).to_broadcast([128, 8, 64]),
                                    ALU.subtract).then_inc(s_sub[j], 1)
                for j in range(CH):
                    v.wait_ge(s_exp[j], n1)
                    v.tensor_reduce(den[:, j], prob[:, j], AX_X, ALU.add).then_inc(s_sum[j], 1)
                    v.wait_ge(s_sum[j], n1)
                    v.reciprocal(rden[:, j], den[:, j]).then_inc(s_rec[j], 1)

            def layer_norm(m1):
                for k in range(TILES // 2):
                    v.wait_ge(f_sb[k], m1)
                    for tl in (2 * k, 2 * k + 1):
                        for a in range(2):
                            st = v.bn_stats(stats[:, tl, a, :], ff[:, tl, a * C:a * C + C])
                st.then_inc(stat_ok, 1)
                v.wait_ge(stat_ok, m1)
                v.tensor_tensor(dmean[:], stats[:, :, :, 1], stats[:, :, :, 4], ALU.subtract).then_inc(dm_ok, 1)
                v.tensor_tensor(msum[:], stats[:, :, :, 2], stats[:, :, :, 5], ALU.add).then_inc(dm_ok, 1)
                v.wait_ge(dm_ok, m1 + m1)
                v.scalar_tensor_tensor(out=dsq[:], in0=dmean[:], scalar=0.25, in1=dmean[:], op0=ALU.mult,
                                       op1=ALU.mult).then_inc(q_ok, 1)
                v.tensor_scalar(msum[:], msum[:], 1.0 / C, LN_EPS, ALU.mult, ALU.add).then_inc(ve_ok, 1)
                v.wait_ge(q_ok, m1)
                v.wait_ge(ve_ok, m1)
                v.tensor_tensor(vare[:], dsq[:], msum[:], ALU.add).then_inc(var_ok, 1)
                v.wait_ge(rstd_ok, m1)
                v.tensor_tensor(act_h[:].rearrange("p t (a c) -> p (t a) c", a=2),
                                ff[:, :, 128:256].rearrange("p t (a c) -> p t a c", a=2),
                                rstd[:].unsqueeze(3).to_broadcast([128, TILES, 2, C]), ALU.mult).then_inc(hmul, 1)

            def residual(n1, par):
                for q in range(2):
                    v.wait_ge(a_ps[q], n1)
                    for odd in range(2):
                        def at(tile, pad):
                            c0 = pad + q * HALF
                            return tile[:, pad:pad + WS, c0:c0 + HALF].rearrange(
                                "c h (k o w) -> c h k o w", o=2, w=WS)[:, :, :, odd, :]
                        r = v.tensor_tensor(at(x1, 0), acc[odd][:].rearrange("c (h k w) -> c h k w", h=WS, w=WS),
                                            at(xt[par], 1), ALU.add)
                    r.then_inc(x1_sb[q], 1)

            def reorder(n1, u48, par):
                v.wait_ge(x_in[par], u48)
                for j in range(CH):
                    v.tensor_copy(xw[:, 8 * j:8 * j + 8].rearrange("c k (h w) -> c k h w", w=WS),
                                  xt[par][:, 1:1 + WS, 1 + j * 64:65 + j * 64].rearrange("c h (k w) -> c k h w", w=WS))\
                        .then_inc(xw_sb[j], 1)

            def attention(n1, u48, par):
                reorder(n1, u48, par)
                values(n1)
                softmax(n1)

            v.sem_inc(x1_sb[1], 2)
            v.sem_inc(x1_sb[0], 2)
            with v.Fori(0, PAIRS) as pair:
                n0 = v.snap(pair * STRIPS + 1)
                v.tensor_copy(val_w[:], val_w_all[:, bass.ds(pair, 1), :].rearrange("c o w -> c (o w)"))
                v.tensor_copy(val_b[:], val_b_all[:, bass.ds(pair, 1), :].rearrange("c o w -> c (o w)"))\
                    .then_inc(pair_w, 1)
                v.wait_ge(pair_w, pair + 1)
                u0 = v.snap(pair * (48 * STRIPS // 2) + 48)
                attention(n0, u0, 0)
                residual(n0, 0)
                with v.Fori(0, STRIPS // 2 - 1) as i:
                    for j in range(2):
                        n1 = v.snap(n0 + i * 2 + (1 + j))
                        attention(n1, v.snap(u0 + i * 48 + 48 * j), (1 + j) % 2)
                        layer_norm(v.snap(n1 - 1))
                        residual(n1, (1 + j) % 2)
                last = v.snap(n0 + (STRIPS - 1))
                attention(last, v.snap(u0 + 48 * (STRIPS // 2 - 1)), 1)
                layer_norm(v.snap(last - 1))
                residual(last, 1)
                layer_norm(last)

        @block.tensor
        def _(p):
            def mm(o, l, r, start=True, stop=True):
                return p.matmul(o, l, r, start=start, stop=stop, skip_group_check=True)

            def project(n1):
                for j in range(CH):
                    if j >= 2:
                        p.wait_ge(g_sb[j - 2], n1)
                    p.wait_ge(xw_sb[j], n1)
                    mm(proj[j % 2][:], g_w[:], xw[:, 8 * j:8 * j + 8].rearrange("c k w -> c (k w)")).then_inc(g_ps[j], 1)
                for j in range(CH):
                    if j < 2:
                        p.wait_ge(g_sb[j + 2], n1)
                    else:
                        p.wait_ge(v_sb[j - 2], n1)
                    for k in range(4):
                        w = 8 * j + 2 * k
                        last = mm(proj[j % 2][:, 128 * k:128 * k + 128],
                                  xw[:, w:w + 2].rearrange("c k w -> c (k w)"),
                                  val_w[:])
                    last.then_inc(v_ps[j], 1)

            def convolve(n1, par, q):
                x = xt[par]
                for r in range(4):
                    for dx in range(3):
                        last = mm(wide[q][:], conv_w[:, 3 * r + dx, :],
                                  x[:, r:r + 7:2, dx + q * HALF:dx + q * HALF + HALF],
                                  r == 0 and dx == 0, r == 3 and dx == 2)
                last.then_inc(c_ps[q], 1)

            def scores(n1):
                for j in range(CH):
                    p.wait_ge(g_sb[j], n1)
                    if j >= 2:
                        p.wait_ge(s_sub[j - 2], n1)
                    p.sem_inc(waited, 1)
                    for k in range(8):
                        for a in range(2):
                            lo = a * C
                            last = mm(scr[j % 2][lo:lo + C, 64 * k:64 * k + 64], g[lo:lo + C, 8 * j + k], xw[lo:lo + C, 8 * j + k])
                    last.then_inc(s_ps[j], 1)

            def transposes(n1):
                for j in range(CH):
                    p.wait_ge(s_nrm[j], n1)
                    if j < 2:
                        p.wait_ge(v_sb[j + 2], n1)
                    else:
                        p.wait_ge(t_sb[j - 2], n1)
                    for k in range(4):
                        last = p.transpose(proj[j % 2][:, 128 * k:128 * k + 128],
                                           prob[:, j, 2 * k:2 * k + 2, :].rearrange("c k s -> c (k s)"), ident[:])
                    last.then_inc(t_ps[j], 1)

            def combine(n1, q):
                if q == 0:
                    p.wait_ge(c_sb[0], n1)
                    p.wait_ge(c_sb[1], n1)
                else:
                    p.wait_ge(x1_sb[0], n1 + 2)
                for odd in range(2):
                    bank = acc[odd][:].rearrange("c (h k w) -> c h k w", h=WS, w=WS)
                    for par in range(2):
                        mm(bank[:, par:WS:2], ms2_w[:, par, :],
                           hid[:, q].rearrange("c r (k o w) -> c r k o w", o=2, w=WS)[:, :, :, odd, :],
                           par == 0, False)
                for j in (2 * q, 2 * q + 1):
                    p.wait_ge(t_sb[j], n1)
                    p.sem_inc(waited, 1)
                    for k in range(4):
                        for odd, a in ((0, 0), (1, 1), (1, 0), (0, 1)):
                            s, c = slice(odd * 64, odd * 64 + 64), slice(a * C, a * C + C)
                            bank = acc[odd][:].rearrange("c (h k w) -> c h k w", h=WS, w=WS)
                            last = mm(bank[c, :, 4 * (j % 2) + k, :], val[s, j, k, c], probT[s, j, k, c],
                                      False, j % 2 == 1 and k == 3)
                last.then_inc(a_ps[q], 1)

            def token_major(m1, n1):
                for k in range(TILES // 2):
                    if k == 0:
                        p.wait_ge(x1_sb[0], m1 + 2)
                        p.wait_ge(x1_sb[1], m1 + 2)
                    if k < 2:
                        p.wait_ge(s_sub[k + 2], n1)
                    else:
                        p.wait_ge(f_sb[k - 2], m1)
                    for e in range(2):
                        last = mm(scr[k % 2][:, 256 * e:256 * e + 256], x1[:, k, e * HALF:e * HALF + HALF], ffn_w[:])
                    last.then_inc(f_ps[k], 1)

            def components(m1):
                p.wait_ge(hact, m1)
                for r in range(2):
                    for e in range(2):
                        tl = slice(8 * r + e, 8 * r + 8, 2)
                        mm(wide[r][0:COMP, :], colb[:, e, :], ff[:, tl, 0:128], e == 0, e == 1)
                        last = mm(wide[r][64:64 + COMP, :], colb[:, e, :], act_h[:, tl, :], e == 0, e == 1)
                    last.then_inc(z_ps[r], 1)

            def attention(n1, u48, par, z1):
                p.wait_ge(x_in[par], u48)
                p.wait_ge(z_sb[0], z1)
                convolve(n1, par, 0)
                project(n1)
                scores(n1)
                p.wait_ge(z_sb[1], z1)
                convolve(n1, par, 1)

            def finish(n1):
                transposes(n1)
                combine(n1, 0)
                combine(n1, 1)

            p.wait_ge(consts_in, 16)
            with p.Fori(0, PAIRS) as pair:
                n0 = p.snap(pair * STRIPS + 1)
                u0 = p.snap(pair * (48 * STRIPS // 2) + 48)
                p.wait_ge(pair_w, pair + 1)
                attention(n0, u0, 0, n0)
                finish(n0)
                with p.Fori(0, STRIPS // 2 - 1) as i:
                    for j in range(2):
                        n1 = p.snap(n0 + i * 2 + (1 + j))
                        m1 = p.snap(n1 - 1)
                        attention(n1, p.snap(u0 + i * 48 + 48 * j), (1 + j) % 2, m1)
                        token_major(m1, n1)
                        finish(n1)
                        components(m1)
                last = p.snap(n0 + (STRIPS - 1))
                before = p.snap(last - 1)
                attention(last, p.snap(u0 + 48 * (STRIPS // 2 - 1)), 1, before)
                token_major(before, last)
                finish(last)
                components(before)
                p.wait_ge(z_sb[0], last)
                p.wait_ge(z_sb[1], last)
                token_major(last, last)
                components(last)


def modes_and_output(nc, t, comps, out, blur_b, keep):
    with ExitStack() as ctx:
        def sb(name, shape):
            return ctx.enter_context(nc.sbuf_tensor(name, shape, F32))

        def sem(name):
            return ctx.enter_context(nc.semaphore(name))

        fc2_w, same_w, fc2_b = keep["fc2_w"], keep["same_w"], keep["fc2_b"]
        w1 = t["w1"]
        rowb = sb("rowb", [128, 2, M, 2, M])
        xx = sb("xx", [128, M, M, B])
        banks = [ctx.enter_context(nc.psum_tensor(f"tb{i}", [128, BANK], F32)) for i in range(8)]

        consts = sem("tail_consts")
        with ExitStack() as c2:
            comp_in = [c2.enter_context(nc.sbuf_tensor(f"comp_in{i}", [128, COMP, 2, 128], F32)) for i in range(2)]
            dsb = c2.enter_context(nc.sbuf_tensor("dsb", [128, 2, MM], F32))
            loaded = [c2.enter_context(nc.semaphore(f"loaded{i}")) for i in range(2)]
            d_ps, d_sb, u_ps, u_sb = (c2.enter_context(nc.semaphore(n)) for n in ("d_ps", "d_sb", "u_ps", "u_sb"))
            block = c2.enter_context(nc.Block())

            @block.sync
            def _(sp):
                sp.dma_start(rowb[:].rearrange("p a b c d -> p (a b c d)"), t["k_rowb"]).then_inc(consts, 16)
                with sp.Fori(0, PAIRS) as pair:
                    sp.wait_ge(d_ps, pair + 1)
                    for half in range(2):
                        sp.dma_start(comp_in[half][:], comps[pair, half * 128:half * 128 + 128])\
                            .then_inc(loaded[half], 16)

            @block.tensor
            def _(p):
                p.sem_inc(d_ps, 1)
                p.wait_ge(consts, 16)
                with p.Fori(0, PAIRS) as pair:
                    n1 = p.snap(pair + 1)
                    p.wait_ge(d_sb, n1)
                    for half in range(2):
                        p.wait_ge(loaded[half], n1 * 16)
                        for part in range(2):
                            for k2 in range(M):
                                for cs in range(2):
                                    last = p.matmul(banks[part][:, k2 * M:k2 * M + M],
                                                    comp_in[half][:, cs * M + k2, part, :], rowb[:, half, k2, cs, :],
                                                    start=half == 0 and k2 == 0 and cs == 0,
                                                    stop=half == 1 and k2 == M - 1 and cs == 1, skip_group_check=True)
                    last.then_inc(d_ps, 1)
                    p.wait_ge(d_sb, n1 + 1)
                    p.wait_ge(u_sb, n1)
                    for a in range(2):
                        p.matmul(banks[2 + a][:, 0:MM], fc2_w[:, a, :], dsb[:, 1, :], start=True, stop=False,
                                 skip_group_check=True)
                        last = p.matmul(banks[2 + a][:, 0:MM], same_w[:, a, :], dsb[:, 0, :], start=False, stop=True,
                                        skip_group_check=True)
                    last.then_inc(u_ps, 1)

            @block.vector
            def _(v):
                v.sem_inc(d_sb, 1)
                v.sem_inc(u_sb, 1)
                with v.Fori(0, PAIRS) as pair:
                    n1 = v.snap(pair + 1)
                    v.wait_ge(d_ps, n1 + 1)
                    for part in range(2):
                        last = v.tensor_copy(dsb[:, part, :].rearrange("c (i j) -> c i j", i=M),
                                             banks[part][:, 0:MM].rearrange("c (j i) -> c i j", i=M))
                    last.then_inc(d_sb, 1)
                    v.wait_ge(u_ps, n1)
                    for a in range(2):
                        at = v.snap(pair * 2 + a)
                        src = banks[2 + a][:, 0:MM].rearrange("c (i j) -> c i j", i=M)
                        dst = xx[:, :, :, bass.ds(at, 1)].rearrange("c i j o -> c i (j o)")
                        v.tensor_copy(dst[0:C], src[0:C])
                        for di, si in ((slice(0, 1), slice(0, 1)), (slice(1, M), slice(M - 1, 0, -1))):
                            for dj, sj in ((slice(0, 1), slice(0, 1)), (slice(1, M), slice(M - 1, 0, -1))):
                                last = v.tensor_copy(dst[C:128, di, dj], src[C:128, si, sj])
                    last.then_inc(u_sb, 1)

        P2 = M + 2
        ypad = sb("ypad", [C, B, P2, P2])
        yblur = sb("yblur", [C, B, P2, P2])

        with ExitStack() as c2:
            def sb2(name, shape):
                return c2.enter_context(nc.sbuf_tensor(name, shape, F32))

            def sem2(name):
                return c2.enter_context(nc.semaphore(name))

            wa = [sb2(f"wa{i}", [128, C, M]) for i in range(2)]
            wn = [sb2(f"wn{i}", [128, C, M]) for i in range(2)]
            wm = [sb2(f"wm{i}", [128, C, M]) for i in range(2)]
            sign = sb2("sign", [128, 1])
            w_in = [sem2(f"w_in{i}") for i in range(2)]
            w_ok, m_ps, m_sb = sem2("w_ok"), sem2("m_ps"), sem2("m_sb")
            setup, bias_ok, blur_pass = sem2("setup"), sem2("bias_ok"), sem2("blur_pass")
            block = c2.enter_context(nc.Block())

            @block.sync
            def _(sp):
                for i in range(M):
                    if i >= 2:
                        sp.wait_ge(w_ok, i - 1)
                    for lo in (0, C):
                        sp.dma_start(wa[i % 2][lo:lo + C], w1[:, :, i, :]).then_inc(w_in[i % 2], 16)
                        sp.dma_start(wn[i % 2][lo:lo + C], w1[:, :, (M - i) % M, :]).then_inc(w_in[i % 2], 16)

            @block.vector
            def _(v):
                def mixed(i):
                    v.wait_ge(m_ps, i + 1)
                    v.tensor_copy(ypad[:, :, i + 1, 1:M + 1],
                                  banks[i % 4][0:C, 0:M * B].rearrange("c (j b) -> c b j", b=B)).then_inc(m_sb, 1)

                v.memset(sign[0:C], 1.0)
                v.memset(sign[C:128], -1.0)
                v.memset(ypad[:], 0.0).then_inc(setup, 1)
                v.wait_ge(setup, 1)
                v.tensor_scalar(xx[:, 0, 0, :], xx[:, 0, 0, :], fc2_b[:], None, ALU.add).then_inc(bias_ok, 1)
                for i in range(M):
                    k = i % 2
                    v.wait_ge(w_in[k], 64 * (i // 2 + 1))
                    if i >= 2:
                        v.wait_ge(m_ps, i - 1)
                    v.scalar_tensor_tensor(out=wm[k][:, :, 0:1], in0=wn[k][:, :, 0:1], scalar=sign[:],
                                           in1=wa[k][:, :, 0:1], op0=ALU.mult, op1=ALU.add)
                    v.scalar_tensor_tensor(out=wm[k][:, :, 1:M], in0=wn[k][:, :, M - 1:0:-1], scalar=sign[:],
                                           in1=wa[k][:, :, 1:M], op0=ALU.mult, op1=ALU.add).then_inc(w_ok, 1)
                    if i >= 1:
                        mixed(i - 1)
                mixed(M - 1)
                v.wait_ge(m_sb, M)
                for s in range(B):
                    if s:
                        v.wait_ge(blur_pass, s)
                    for b in range(B):
                        src, dst = ypad[:, s].rearrange("c i j -> c (i j)"), yblur[:, b].rearrange("c i j -> c (i j)")
                        if s == 0:
                            last = v.tensor_scalar(dst, src, float(blur_b[b, s]), None, ALU.mult)
                        elif blur_b[b, s] != 0.0:
                            last = v.scalar_tensor_tensor(out=dst, in0=src, scalar=float(blur_b[b, s]), in1=dst,
                                                          op0=ALU.mult, op1=ALU.add)
                    last.then_inc(blur_pass, 1)

            @block.tensor
            def _(p):
                p.wait_ge(bias_ok, 1)
                for i in range(M):
                    p.wait_ge(w_ok, i + 1)
                    if i >= 4:
                        p.wait_ge(m_sb, i - 3)
                    for j in range(M):
                        last = p.matmul(banks[i % 4][0:C, j * B:j * B + B], wm[i % 2][:, :, j], xx[:, i, j, :],
                                        start=True, stop=True)
                    last.then_inc(m_ps, 1)

        with ExitStack() as c2:
            def sb2(name, shape):
                return c2.enter_context(nc.sbuf_tensor(name, shape, F32))

            def sem2(name):
                return c2.enter_context(nc.semaphore(name))

            def sems2(name, n):
                return [sem2(f"{name}{i}") for i in range(n)]

            GO = 4
            GROUPS = C // GO
            DEEP = 4
            ycur = sb2("ycur", [C, P2, P2])
            blurc = sb2("blurc", [C, C])
            inv = sb2("inv", [128, H])
            invc = sb2("invc", [64, 2, KEPT])
            tcur = sb2("tcur", [64, 32, C])
            rr = [sb2(f"rr{i}", [128, 2 * KEPT]) for i in range(2)]
            stage = [[sb2(f"stage{i}_{hh}", [128, GO, W]) for hh in range(2)] for i in range(DEEP)]
            tail_in, clear = sem2("tail_in"), sem2("clear")
            waited = sem2("waited_tail")
            y_sb, t_ps, t_sb = sem2("y_sb"), sem2("t_ps"), sem2("t_sb")
            r_ps, r_sb = sem2("r_ps"), sem2("r_sb")
            o_ps = sems2("o_ps", 2)
            o_sb = sems2("o_sb", 2)
            stored = [sems2(f"stored{hh}_", DEEP) for hh in range(2)]
            block = c2.enter_context(nc.Block())

            def evacuate(eng, copy, b, n16, g, hh):
                slot = g % DEEP
                eng.wait_ge(o_ps[hh], n16 + g)
                eng.wait_ge(stored[hh][slot], (b * (GROUPS // DEEP) + (g // DEEP + 1)) * 16)
                for oo in range(2):
                    src = banks[4 + 2 * hh + oo][:, 0:2 * KEPT].rearrange("h (o w) -> h o w", w=KEPT)
                    copy(stage[slot][hh][:, oo:GO:2, 0:KEPT_LO], src[:, :, 0:KEPT_LO])
                    last = copy(stage[slot][hh][:, oo:GO:2, W - KEPT_HI:W], src[:, :, KEPT_LO:KEPT])
                last.then_inc(o_sb[hh], 1)

            @block.sync
            def _(sp):
                for dst, src in ((blurc[:], t["k_blurc"]), (inv[:], t["k_inv"]), (invc[:], t["k_invc"])):
                    sp.dma_start(dst, src).then_inc(tail_in, 16)
                with sp.Fori(0, B) as b:
                    n16 = sp.snap(b * GROUPS + 2)
                    for g in range(GROUPS):
                        for hh in range(2):
                            sp.wait_ge(o_sb[hh], n16 + g)
                            sp.dma_start(out[b, g * GO:g * GO + GO, hh * 128:hh * 128 + 128, :]
                                         .rearrange("o h w -> h o w"), stage[g % DEEP][hh][:])\
                                .then_inc(stored[hh][g % DEEP], 16)
                for hh in range(2):
                    for slot in range(DEEP):
                        sp.wait_ge(stored[hh][slot], 16 * (B * GROUPS // DEEP + 1))

            @block.vector
            def _(v):
                v.memset(tcur[:], 0.0)
                for slot in range(DEEP):
                    for hh in range(2):
                        last = v.memset(stage[slot][hh][:], 0.0)
                last.then_inc(clear, 1)
                v.sem_inc(o_sb[1], 1)
                for slot in range(DEEP):
                    v.sem_inc(stored[1][slot], 16)
                v.wait_ge(clear, 1)
                with v.Fori(0, B) as b:
                    n1 = v.snap(b + 1)
                    n16 = v.snap(b * GROUPS + 1)
                    v.tensor_copy(ycur[:], yblur[:, bass.ds(b, 1)].rearrange("c o i j -> c (o i) j")).then_inc(y_sb, 1)
                    for c in range(3):
                        v.wait_ge(t_ps, b * 3 + (c + 1))
                        for q in (0, 32):
                            last = v.tensor_copy(tcur[q:q + M1, 7 * c:7 * c + 7, :],
                                                 banks[c % 2][q:q + M1, 0:7 * C].rearrange("q (m o) -> q m o", o=C))
                        last.then_inc(t_sb, 1)
                    for g in range(GROUPS):
                        evacuate(v, v.tensor_copy, b, n16, g, 1)

            @block.scalar
            def _(sc):
                def copy(dst, src):
                    return sc.activation(dst, src, ACT.Identity)

                sc.sem_inc(o_sb[0], 1)
                for slot in range(DEEP):
                    sc.sem_inc(stored[0][slot], 16)
                sc.wait_ge(clear, 1)
                with sc.Fori(0, B) as b:
                    n16 = sc.snap(b * GROUPS + 1)
                    for g in range(GROUPS + 1):
                        if g < GROUPS:
                            sc.wait_ge(r_ps, n16 + g)
                            copy(rr[g % 2][:], banks[2 + g % 2][:, 0:2 * KEPT]).then_inc(r_sb, 1)
                        if g >= 1:
                            evacuate(sc, copy, b, n16, g - 1, 0)

            @block.tensor
            def _(p):
                p.wait_ge(tail_in, 48)
                p.wait_ge(clear, 1)
                with p.Fori(0, B) as b:
                    n1 = p.snap(b + 1)
                    n16 = p.snap(b * GROUPS + 1)
                    p.wait_ge(y_sb, n1)
                    p.sem_inc(waited, 1)
                    for c in range(3):
                        if c == 2:
                            p.wait_ge(t_sb, b * 3 + 1)
                            p.sem_inc(waited, 1)
                        for m in range(7 * c, 7 * c + 7):
                            for q, y in ((0, ycur[:, m + 1, 1:1 + M1]), (32, ycur[:, m, 0:M1])):
                                last = p.matmul(banks[c % 2][q:q + M1, (m - 7 * c) * C:(m - 7 * c) * C + C], y,
                                                blurc[:], start=True, stop=True)
                        last.then_inc(t_ps, 1)
                    p.wait_ge(t_sb, b * 3 + 3)
                    p.sem_inc(waited, 1)
                    for g in range(GROUPS + 1):
                        if g < GROUPS:
                            for c in range(2):
                                for oo in range(2):
                                    for cs in range(2):
                                        q = 64 * oo + 32 * cs
                                        last = p.matmul(banks[2 + g % 2][q:q + 32, c * KEPT:c * KEPT + KEPT],
                                                        tcur[:, :, g * GO + 2 * c + oo], invc[:, cs, :],
                                                        start=True, stop=True, tile_position=(0, q))
                            last.then_inc(r_ps, 1)
                        if g >= 1:
                            k = g - 1
                            p.wait_ge(r_sb, n16 + k)
                            for hh in range(2):
                                p.wait_ge(o_sb[hh], n16 + k)
                                for oo in range(2):
                                    s = slice(64 * oo, 64 * oo + 64)
                                    last = p.matmul(banks[4 + 2 * hh + oo][:, 0:2 * KEPT],
                                                    inv[s, hh * 128:hh * 128 + 128], rr[k % 2][s, :],
                                                    start=True, stop=True)
                                last.then_inc(o_ps[hh], 1)


_LAYER0 = ["qk_w", "qk_b", "v_w", "v_b", "out_w", "out_b", "ms1_w", "ms1_b", "ms2_w", "ms2_b", "se1_w", "se1_b",
           "se2_w", "se2_b", "ln_g", "ln_b", "fc1_w", "fc1_b", "fc2_w", "fc2_b"]


def kernel(**inputs):
    import concourse.bacc as _bacc
    from concourse.bass_utils import run_bass_kernel_spmd as _run

    nc = _bacc.Bacc("TRN2", target_bir_lowering=False, num_devices=1)
    arrays, tensors = {}, {}
    given = {"x": inputs["x"], "w1": inputs["L1_conv_w1"]}
    given.update({name: inputs["L0_conv_" + name] for name in _LAYER0})
    tables = {name: a.astype(np.float32) for name, a in shape_constants().items()}
    for name, a in list(given.items()) + list(tables.items()):
        a = np.ascontiguousarray(a)
        arrays[f"in_{name}"] = a
        tensors[name] = nc.dram_tensor(f"in_{name}", a.shape, F32, kind="ExternalInput").ap()
    out = nc.dram_tensor("out_0", (B, C, H, W), F32, kind="ExternalOutput").ap()
    conv_layer_then_hartley_kernel(nc, tensors, out)
    r = _run(nc, [arrays], core_ids=[0])
    return r.results[0]["out_0"]
```

```python
from contextlib import ExitStack

import numpy as np
import concourse.bass as bass
from concourse import mybir

F32 = mybir.dt.float32
ALU = mybir.AluOpType
ACT = mybir.ActivationFunctionType
AX_X = mybir.AxisListType.X

B, C, H, W = 8, 64, 256, 256
PAIRS = B // 2
WS = 8
STRIPS = H // WS
WIN = W // WS
HALF = W // 2
PX = WS * W
HID = C // 2
SE = C // 16
M = 20
MM = M * M
COMP = 2 * M
M1 = M + 1
KEPT_LO, KEPT_HI = 65, 64
KEPT = KEPT_LO + KEPT_HI
SCALE = 1.0 / C ** 0.5
LN_EPS = 1e-5
CH = 4
BANK = 512


def blur_matrix(n, sigma=1.0, radius=4):
    t = np.arange(-radius, radius + 1, dtype=np.float32)
    k = np.exp(-0.5 * (t / sigma) ** 2)
    k = (k / k.sum()).astype(np.float64)
    g = np.zeros((n, n))
    for i in range(n):
        for j in range(2 * radius + 1):
            g[i, min(max(i + j - radius, 0), n - 1)] += k[j]
    return g


def shape_constants():
    two_pi = 2 * np.pi
    ident = np.eye(128)
    ang = two_pi * np.outer(np.arange(W), np.arange(M)) / W
    colb = np.concatenate([np.cos(ang), np.sin(ang)], 1).reshape(2, 128, COMP).transpose(1, 0, 2)
    h = np.arange(H)[:, None, None]
    k2 = np.arange(M)[None, :, None]
    k1 = np.arange(M)[None, None, :]
    a1 = two_pi * h * k1 / H
    phi = two_pi * (k1 + k2) / H
    rowb = np.stack([np.cos(a1) - np.sin(a1 + phi), -np.sin(a1) - np.cos(a1 + phi)], 2)
    rowb = rowb.reshape(2, 128, M, 2, M).transpose(1, 0, 2, 3, 4)
    m = np.arange(M1)
    inv = np.zeros((2, 32, H))
    inv[0, :M1] = np.cos(two_pi * np.outer(m, np.arange(H)) / H)
    inv[1, :M1] = np.sin(two_pi * np.outer(m, np.arange(H)) / H)
    inv = (inv.reshape(64, H) @ blur_matrix(H).T) * (0.5 / (H * W))
    inv = np.concatenate([inv, inv], 0)
    keep = np.r_[0:KEPT_LO, W - KEPT_HI:W]
    c = np.cos(two_pi * np.outer(m, np.arange(W)) / W)
    s = np.sin(two_pi * np.outer(m, np.arange(W)) / W)
    invc = np.zeros((64, 2, W))
    invc[0:M1, 0], invc[32:32 + M1, 0], invc[0:M1, 1], invc[32:32 + M1, 1] = c, -s, -s, -c
    invc = (invc @ blur_matrix(W).T)[:, :, keep]
    center = np.eye(C) - 1.0 / C
    return {
        "k_ident": ident, "k_colb": colb, "k_rowb": rowb.reshape(128, -1), "k_inv": inv,
        "k_invc": invc, "k_center": np.concatenate([center, center], 1), "k_blurc": blur_matrix(C).T,
    }


def conv_layer_then_hartley_kernel(nc, t, out):
    x_pair = t["x"].rearrange("(p a) c h w -> p (a c) h w", a=2)
    blur_b = blur_matrix(B)
    comps = nc.dram_tensor("mode_columns", [PAIRS, H, COMP, 2, 2 * C], F32, kind="Internal").ap()

    top = ExitStack()
    with top:
        def keep_sb(name, shape):
            return top.enter_context(nc.sbuf_tensor(name, shape, F32))

        ident = keep_sb("ident", [128, 128])
        g_w = keep_sb("g_w", [128, 128])
        g_b = keep_sb("g_b", [128, 1])
        val_w_all = keep_sb("val_w_all", [128, PAIRS, 128])
        val_b_all = keep_sb("val_b_all", [128, PAIRS, 128])
        conv_w = keep_sb("conv_w", [128, 2, 2, 3, HID])
        conv_b = keep_sb("conv_b", [128, 1])
        ms2_w = keep_sb("ms2_w", [128, 2, 128])
        ffn_w = keep_sb("ffn_w", [128, 128])
        ffn_b = keep_sb("ffn_b", [128, 128])
        fc2_w = keep_sb("fc2_w", [128, 2, 128])
        same_w = keep_sb("same_w", [128, 2, 128])
        fc2_b = keep_sb("fc2_b", [128, 1])

        prepare(nc, t, x_pair, locals())
        main(nc, t, x_pair, comps, locals())
        modes_and_output(nc, t, comps, out, blur_b, locals())


def prepare(nc, t, x_pair, keep):
    with ExitStack() as ctx:
        def sb(name, shape):
            return ctx.enter_context(nc.sbuf_tensor(name, shape, F32))

        def sem(name):
            return ctx.enter_context(nc.semaphore(name))

        ident, g_w, g_b = keep["ident"], keep["g_w"], keep["g_b"]
        val_w_all, val_b_all = keep["val_w_all"], keep["val_b_all"]
        conv_w, conv_b, ms2_w = keep["conv_w"], keep["conv_b"], keep["ms2_w"]
        ffn_w, ffn_b, fc2_w, same_w, fc2_b = (keep[k] for k in ("ffn_w", "ffn_b", "fc2_w", "same_w", "fc2_b"))

        PIECE = 32
        PIECES = H // PIECE
        xs = sb("xs", [128, 2, PIECE * W])
        junk = sb("junk", [128, PIECE * W])
        sums = sb("sums", [128, PAIRS, PIECES])
        gap = sb("gap", [128, PAIRS])
        wq2 = sb("wq2", [C, 2, C])
        wk2 = sb("wk2", [C, 2, C])
        bq = sb("bq", [C, 1])
        vw2 = sb("vw2", [C, 2, C])
        vb = sb("vb", [C, 1])
        ow_t = sb("ow_t", [C, C])
        ob = sb("ob", [C, 1])
        ms1_raw = sb("ms1_raw", [HID, C * 9])
        conv_t = sb("conv_t", [128, 9, HID])
        ms2b_row = sb("ms2b_row", [128, C])
        se1_t = sb("se1_t", [128, SE])
        se1_b = sb("se1_b", [SE, 1])
        se2_t = sb("se2_t", [SE, 2, C])
        se2_b = sb("se2_b", [128, 1])
        fc1_t = sb("fc1_t", [C, C])
        ln_g = sb("ln_g", [C, 1])
        ln_b = sb("ln_b", [C, 1])
        fc1b_row = sb("fc1b_row", [128, C])
        fc2b_raw = sb("fc2b_raw", [128, 1])
        center = sb("center", [C, 128])
        fc1_g = sb("fc1_g", [C, C])
        ln_b_wide = sb("ln_b_wide", [C, 128])
        hidden = sb("hidden", [SE, 2, PAIRS])
        gate = sb("gate", [128, 2, PAIRS])
        gate_wide = sb("gate_wide", [C, 2 * PAIRS, 128])
        gate_row = sb("gate_row", [128, 2, PAIRS, C])
        obv = sb("obv", [C, 1])
        obv_wide = sb("obv_wide", [C, 128])
        obv_row = sb("obv_row", [128, C])
        vw_plain = sb("vw_plain", [128, C])
        pA = ctx.enter_context(nc.psum_tensor("pA", [128, BANK], F32))
        pB = ctx.enter_context(nc.psum_tensor("pB", [128, BANK], F32))
        pC = ctx.enter_context(nc.psum_tensor("pC", [128, BANK], F32))
        pD = ctx.enter_context(nc.psum_tensor("pD", [128, BANK], F32))

        weights_in, zeroed, placed = sem("weights_in"), sem("zeroed"), sem("placed")
        piece_in = [sem("piece_in0"), sem("piece_in1")]
        piece_sum = sem("piece_sum")
        dve, pe, act = sem("dve_step"), sem("pe_step"), sem("act_step")

        def vec(name):
            return t[name].rearrange("(c o) -> c o", o=1)

        loads = [
            (ident[:], t["k_ident"]), (center[:], t["k_center"]),
            (bq[:], vec("qk_b")[0:C]), (vb[:], vec("v_b")), (ob[:], vec("out_b")),
            (ms1_raw[:], t["ms1_w"].rearrange("o c kh kw -> o (c kh kw)")),
            (ms2b_row[:], t["ms2_b"].partition_broadcast(128)),
            (fc1b_row[:], t["fc1_b"].partition_broadcast(128)),
            (se1_b[:], vec("se1_b")), (ln_g[:], vec("ln_g")), (ln_b[:], vec("ln_b")),
            (fc1_t[:], t["fc1_w"].rearrange("o c -> c o")),
            (ow_t[:], t["out_w"].rearrange("o c -> c o")),
        ]
        for a in range(2):
            lo, hi = a * C, a * C + C
            loads += [
                (wq2[:, a, :], t["qk_w"][0:C, :]), (wk2[:, a, :], t["qk_w"][C:2 * C, :]),
                (vw2[:, a, :], t["v_w"]), (se2_b[lo:hi, :], vec("se2_b")),
                (se1_t[lo:hi, :], t["se1_w"].rearrange("o c -> c o")),
                (se2_t[:, a, :], t["se2_w"].rearrange("o c -> c o")),
                (fc2b_raw[lo:hi, :], vec("fc2_b")),
            ]
            for par in range(2):
                r = par * C + a * HID
                loads += [(conv_b[r:r + HID, :], vec("ms1_b"))]
        late = []
        for a in range(2):
            for par in range(2):
                r = par * C + a * HID
                late += [(ms2_w[r:r + HID, par, a * C:a * C + C], t["ms2_w"].rearrange("o c -> c o"))]
                late += [(fc2_w[a * C:a * C + C, a, par * C:par * C + C], t["fc2_w"].rearrange("o c -> c o")),
                         (same_w[a * C:a * C + C, a, par * C:par * C + C], t["k_ident"][0:C, 0:C])]

        block = ctx.enter_context(nc.Block())

        @block.sync
        def _(sp):
            for q in range(PAIRS * PIECES):
                if q >= 2:
                    sp.wait_ge(piece_sum, q - 1)
                sp.dma_start(xs[:, q % 2, :], x_pair[q // PIECES, :, (q % PIECES) * PIECE:(q % PIECES + 1) * PIECE, :]
                             .rearrange("c h w -> c (h w)")).then_inc(piece_in[q % 2], 16)

        @block.gpsimd
        def _(pool):
            for dst, src in loads:
                pool.dma_start(dst, src, allow_slow_non_contiguous=True).then_inc(weights_in, 16)
            pool.wait_ge(zeroed, 1)
            for dst, src in late:
                pool.dma_start(dst, src, allow_slow_non_contiguous=True).then_inc(placed, 16)
            pool.wait_ge(placed, 16 * len(late))

        @block.scalar
        def _(sc):
            for q in range(PAIRS * PIECES):
                sc.wait_ge(piece_in[q % 2], 16 * (q // 2 + 1))
                if q >= 1:
                    sc.wait_ge(piece_sum, q)
                sc.activation(junk[:], xs[:, q % 2, :], ACT.Copy,
                              accum_out=sums[:, q // PIECES, q % PIECES:q % PIECES + 1]).then_inc(piece_sum, 1)
            sc.wait_ge(pe, 5)
            sc.activation(hidden[:, 0, :], pC[0:SE, 0:PAIRS], ACT.Relu, bias=se1_b[:], scale=1.0 / (H * W))
            sc.activation(hidden[:, 1, :], pB[0:SE, 0:PAIRS], ACT.Relu, bias=se1_b[:], scale=1.0 / (H * W))\
                .then_inc(act, 1)
            sc.wait_ge(pe, 6)
            sc.activation(gate[:], pC[:, 16:16 + 2 * PAIRS].rearrange("c (a p) -> c a p", a=2), ACT.Sigmoid,
                          bias=se2_b[:]).then_inc(act, 1)

        @block.vector
        def _(v):
            steps = [0]

            def link(ins):
                steps[0] += 1
                ins.then_inc(dve, 1)
                v.wait_ge(dve, steps[0])

            for tile in (conv_w, ms2_w, fc2_w, same_w, ffn_w, g_w):
                v.memset(tile[:], 0.0)
            v.memset(val_w_all[:], 0.0).then_inc(zeroed, 1)
            v.wait_ge(zeroed, 1)
            v.wait_ge(weights_in, 16 * len(loads))
            link(v.tensor_scalar(fc1_g[:], fc1_t[:], ln_g[:], None, ALU.mult))
            link(v.tensor_copy(ln_b_wide[:], ln_b[:].to_broadcast([C, 128])))
            v.wait_ge(pe, 1)
            for a in range(2):
                s = slice(a * C, a * C + C)
                v.tensor_scalar(g_w[s, s], pA[s, 0:C], SCALE, None, ALU.mult)
            v.tensor_scalar(g_b[:], pA[:, 2 * C:2 * C + 1], SCALE, None, ALU.mult)
            v.tensor_scalar(fc2_b[:], fc2b_raw[:], float(H * W), None, ALU.mult)
            v.wait_ge(pe, 2)
            link(v.tensor_copy(conv_t[:], pB[:, 0:9 * HID].rearrange("c (k o) -> c k o", k=9)))
            for rp, par, pr, kh in ((1, 0, 0, 0), (0, 0, 1, 1), (1, 0, 1, 2), (0, 1, 0, 0), (1, 1, 0, 1), (0, 1, 1, 2)):
                s = slice(rp * C, rp * C + C)
                v.tensor_copy(conv_w[s, par, pr], conv_t[s, 3 * kh:3 * kh + 3, :])
            v.wait_ge(pe, 3)
            for a in range(2):
                s = slice(a * C, a * C + C)
                v.tensor_copy(ffn_w[s, s], pD[s, 0:C])
                v.tensor_tensor(ffn_b[:, s], pD[:, C:2 * C], fc1b_row[:], ALU.add)
            v.tensor_copy(vw_plain[:], pD[:, 2 * C:3 * C])
            link(v.tensor_tensor(obv[:], pD[0:C, 3 * C:3 * C + 1], ob[:], ALU.add))
            link(v.tensor_copy(obv_wide[:], obv[:].to_broadcast([C, 128])))
            v.wait_ge(pe, 4)
            link(v.tensor_copy(obv_row[:], pD[:, 256:256 + C]))
            v.wait_ge(piece_sum, PAIRS * PIECES)
            link(v.tensor_reduce(gap[:], sums[:], AX_X, ALU.add))
            v.wait_ge(act, 2)
            link(v.tensor_copy(gate_wide[:], gate[0:C].rearrange("c a p -> c (a p)").unsqueeze(2)
                               .to_broadcast([C, 2 * PAIRS, 128])))
            v.wait_ge(pe, 7)
            link(v.tensor_copy(gate_row[:], pA[:, 0:2 * PAIRS * C].rearrange("q (a p c) -> q a p c", a=2, p=PAIRS)))
            for a in range(2):
                s = slice(a * C, a * C + C)
                v.tensor_tensor(val_w_all[s, :, s], gate_row[s, a], vw_plain[s, :].unsqueeze(1)
                                .to_broadcast([C, PAIRS, C]), ALU.mult)
                link(v.tensor_tensor(val_b_all[:, :, s], gate_row[:, a], obv_row[:].unsqueeze(1)
                                     .to_broadcast([128, PAIRS, C]), ALU.mult))
                link(v.tensor_tensor(val_b_all[:, :, s], val_b_all[:, :, s], ms2b_row[:].unsqueeze(1)
                                     .to_broadcast([128, PAIRS, C]), ALU.add))

        @block.tensor
        def _(p):
            def mm(o, l, r, last=False):
                i = p.matmul(o, l, r, start=True, stop=True)
                if last:
                    i.then_inc(pe, 1)

            p.wait_ge(weights_in, 16 * len(loads))
            mm(pA[:, 0:C], wq2[:].rearrange("o a c -> o (a c)"), wk2[:, 0, :])
            mm(pA[:, 2 * C:2 * C + 1], wk2[:].rearrange("o a c -> o (a c)"), bq[:], True)
            raw = ms1_raw[:].rearrange("o (c k) -> o k c", k=9)
            for k in range(9):
                for a in range(2):
                    mm(pB[a * C:a * C + C, k * HID:k * HID + HID], raw[:, k, :], ident[0:HID, 0:HID], k == 8 and a == 1)
            p.wait_ge(dve, 2)
            mm(pD[:, 0:C], center[:], fc1_g[:])
            mm(pD[:, C:2 * C], ln_b_wide[:], fc1_t[:])
            mm(pD[:, 2 * C:3 * C], vw2[:].rearrange("o a c -> o (a c)"), ow_t[:])
            mm(pD[0:C, 3 * C:3 * C + 1], ow_t[:], vb[:], True)
            p.wait_ge(dve, 5)
            mm(pD[:, 256:256 + C], obv_wide[:], ident[0:C, 0:C], True)
            p.wait_ge(dve, 7)
            for a in range(2):
                s = slice(a * C, a * C + C)
                mm((pC, pB)[a][0:SE, 0:PAIRS], se1_t[s, :], gap[s, :], a == 1)
            p.wait_ge(act, 1)
            mm(pC[:, 16:16 + 2 * PAIRS], se2_t[:].rearrange("o a c -> o (a c)"),
               hidden[:].rearrange("c a p -> c (a p)"), True)
            p.wait_ge(dve, 8)
            for i in range(2 * PAIRS):
                mm(pA[:, i * C:i * C + C], gate_wide[:, i, :], ident[0:C, 0:C], i == 2 * PAIRS - 1)


def main(nc, t, x_pair, comps, keep):
    with ExitStack() as ctx:
        def sb(name, shape):
            return ctx.enter_context(nc.sbuf_tensor(name, shape, F32))

        def ps(name):
            return ctx.enter_context(nc.psum_tensor(name, [128, BANK], F32))

        def sem(name):
            return ctx.enter_context(nc.semaphore(name))

        def sems(name, n):
            return [sem(f"{name}{i}") for i in range(n)]

        g_w, g_b, conv_w, conv_b, ms2_w = (keep[k] for k in ("g_w", "g_b", "conv_w", "conv_b", "ms2_w"))
        ffn_w, ffn_b, ident = keep["ffn_w"], keep["ffn_b"], keep["ident"]
        val_w_all, val_b_all = keep["val_w_all"], keep["val_b_all"]

        IN = 7 * 16
        TILES = PX // 128
        xt = [sb(f"xt{i}", [128, WS, W]) for i in range(2)]
        xs = [sb(f"xs{i}", [128, 2, WS // 2 + 2, W + 2]) for i in range(2)]
        zrow = sb("zrow", [128, 2, W])
        val_w = sb("val_w", [128, 128])
        val_b = sb("val_b", [128, 128])
        g = sb("g", [128, WIN, WS * WS])
        xw = sb("xw", [128, WIN, WS * WS])
        xz = sb("xz", [128, WIN, 2, WS * WS])
        val = sb("val", [128, CH, 4, 128])
        prob = sb("prob", [128, CH, 8, 64])
        probT = sb("probT", [128, CH, 4, 2, 128])
        mx = sb("mx", [128, CH, 8])
        den = sb("den", [128, CH, 8])
        rden = sb("rden", [128, CH, 8])
        hid = sb("hid", [128, 2, 4, HALF])
        x1 = sb("x1", [128, WS, W])
        ff = sb("ff", [128, TILES, 256])
        act_h = sb("act_h", [128, TILES, 128])
        stats = sb("stats", [128, TILES, 2, 6])
        dmean = sb("dmean", [128, TILES, 2])
        msum = sb("msum", [128, TILES, 2])
        dsq = sb("dsq", [128, TILES, 2])
        vare = sb("vare", [128, TILES, 2])
        rstd = sb("rstd", [128, TILES, 2])
        minus_half = sb("minus_half", [128, TILES, 2])
        colb = sb("colb", [128, 2, COMP])
        zs = sb("zs", [128, 2, BANK])
        proj = [ps("proj0"), ps("proj1")]
        wide = [ps("wide0"), ps("wide1")]
        acc = [ps("acc0"), ps("acc1")]
        scr = [ps("scr0"), ps("scr1")]

        x_in = sems("x_in", 2)
        consts_in, pads = sem("consts_in"), sem("pads")
        waited = sem("waited")
        pair_w = sem("pair_w")
        xw_sb, xz_sb = sems("xw_sb", CH), sems("xz_sb", CH)
        g_ps, g_sb = sems("g_ps", CH), sems("g_sb", CH)
        v_ps, v_sb = sems("v_ps", CH), sems("v_sb", CH)
        c_ps, c_sb = sems("c_ps", 2), sems("c_sb", 2)
        s_ps, s_max, s_sub = sems("s_ps", CH), sems("s_max", CH), sems("s_sub", CH)
        s_exp, s_sum, s_rec, s_nrm = sems("s_exp", CH), sems("s_sum", CH), sems("s_rec", CH), sems("s_nrm", CH)
        t_ps, t_sb = sems("t_ps", CH), sems("t_sb", CH)
        a_ps, x1_sb = sems("a_ps", CH), sems("x1_sb", CH)
        f_ps, f_sb = sems("f_ps", TILES // 2), sems("f_sb", TILES // 2)
        stat_ok, dm_ok, q_ok, ve_ok, var_ok = sem("stat_ok"), sem("dm_ok"), sem("q_ok"), sem("ve_ok"), sem("var_ok")
        rstd_ok = sem("rstd_ok")
        hmul, hbias, hact = sem("hmul"), sems("hbias", 2), sem("hact")
        z_ps, z_sb = sems("z_ps", 2), sems("z_sb", 2)
        z_out = sem("z_out")

        x_rows = t["x"].rearrange("b c (k r) w -> b r c k w", r=2)
        x_images = t["x"].rearrange("(p a) c h w -> p c a h w", a=2)
        zv = comps.rearrange("p (s r) k m c -> p s m k r c", r=WS)

        block = ctx.enter_context(nc.Block())

        @block.sync
        def _(sp):
            sp.dma_start(colb[:], t["k_colb"]).then_inc(consts_in, 16)
            sp.wait_ge(pads, 4)

            def load(pair, s, n1, par, first=False, last=False):
                sp.wait_ge(x1_sb[CH - 1], n1)
                r0 = s * WS
                sp.dma_start(xt[par][:], x_pair[pair, :, bass.ds(r0, WS), :]).then_inc(x_in[par], 16)
                for a in range(2):
                    own = x_rows[pair * 2 + a]
                    sp.dma_start(xs[par][0:C, a, 1:5, 1:W + 1], own[0, :, bass.ds(s * 4, 4), :])\
                        .then_inc(x_in[par], 16)
                    sp.dma_start(xs[par][C:128, a, 1:5, 1:W + 1], own[1, :, bass.ds(s * 4, 4), :])\
                        .then_inc(x_in[par], 16)
                above, below = xs[par][C:128, :, 0, 1:W + 1], xs[par][0:C, :, 5, 1:W + 1]
                if first:
                    sp.dma_start(above, zrow[C:128]).then_inc(x_in[par], 16)
                else:
                    sp.dma_start(above, x_images[pair, :, :, bass.ds(r0 - 1, 1), :].rearrange("c a h w -> c a (h w)"))\
                        .then_inc(x_in[par], 16)
                if last:
                    sp.dma_start(below, zrow[0:C]).then_inc(x_in[par], 16)
                else:
                    sp.dma_start(below, x_images[pair, :, :, bass.ds(r0 + WS, 1), :].rearrange("c a h w -> c a (h w)"))\
                        .then_inc(x_in[par], 16)

            with sp.Fori(0, PAIRS) as pair:
                n0 = sp.snap(pair * STRIPS + 1)
                load(pair, 0, n0, 0, first=True)
                with sp.Fori(0, STRIPS // 2 - 1) as i:
                    for j in range(2):
                        s = sp.snap(i * 2 + (1 + j))
                        load(pair, s, sp.snap(n0 + s), (1 + j) % 2)
                load(pair, STRIPS - 1, sp.snap(n0 + (STRIPS - 1)), 1, last=True)

        @block.gpsimd
        def _(pool):
            pool.memset(minus_half[:], -0.5)

            def attention(n1):
                for j in range(CH):
                    pool.wait_ge(s_rec[j], n1)
                    pool.tensor_tensor(prob[:, j], prob[:, j], rden[:, j].unsqueeze(2).to_broadcast([128, 8, 64]),
                                       ALU.mult).then_inc(s_nrm[j], 1)

            def feed_forward(m1):
                pool.wait_ge(var_ok, m1)
                pool.tensor_tensor(rstd[:], vare[:], minus_half[:], ALU.pow).then_inc(rstd_ok, 1)

            def strips(eng):
                with eng.Fori(0, PAIRS) as pair:
                    n0 = eng.snap(pair * STRIPS + 1)
                    attention(n0)
                    with eng.Fori(1, STRIPS) as s:
                        attention(eng.snap(n0 + s))
                        feed_forward(eng.snap(n0 + s - 1))
                    feed_forward(eng.snap(n0 + (STRIPS - 1)))

            strips(pool)

        @block.scalar
        def _(sc):
            def attention(n1, before=None):
                relu(n1, 0)
                if before:
                    components(*before)
                for j in range(CH):
                    sc.wait_ge(g_ps[j], n1)
                    sc.activation(g[:, 8 * j:8 * j + 8].rearrange("c k w -> c (k w)"), proj[j % 2][:],
                                  ACT.Identity, bias=g_b[:]).then_inc(g_sb[j], 1)
                for j in range(CH):
                    sc.wait_ge(s_sub[j], n1)
                    sc.activation(prob[:, j], prob[:, j], ACT.Exp).then_inc(s_exp[j], 1)
                relu(n1, 1)

            def relu(n1, q):
                sc.wait_ge(c_ps[q], n1)
                sc.activation(hid[:, q], wide[q][:].rearrange("c (r w) -> c r w", r=4), ACT.Relu,
                              bias=conv_b[:]).then_inc(c_sb[q], 1)

            def transposed(n1):
                for j in range(CH):
                    sc.wait_ge(t_ps[j], n1)
                    for e in range(2):
                        rows = slice(64 * e, 64 * e + 64)
                        last = sc.activation(probT[rows, j, :, :, rows],
                                             proj[j % 2][rows].rearrange("c (r o w) -> c r o w", r=4, o=2), ACT.Identity)
                    last.then_inc(t_sb[j], 1)

            def token_major(m1):
                for k in range(TILES // 2):
                    sc.wait_ge(f_ps[k], m1)
                    sc.activation(ff[:, 2 * k:2 * k + 2, :], scr[k % 2][:].rearrange("c (r w) -> c r w", r=2),
                                  ACT.Identity).then_inc(f_sb[k], 1)

            def gelu(m1):
                for k in range(2):
                    tl = slice(k * TILES // 2, (k + 1) * TILES // 2)
                    sc.wait_ge(hbias[k], m1)
                    last = sc.activation(act_h[:, tl], act_h[:, tl], ACT.Gelu_apprx_tanh)
                last.then_inc(hact, 1)

            def components(pair, s, m1, m32):
                for r in range(2):
                    sc.wait_ge(z_ps[r], m1)
                    if r == 0:
                        sc.wait_ge(z_out, m32)
                    sc.activation(zs[0:COMP, r, :], acc[r][0:COMP, :], ACT.Identity)
                    sc.activation(zs[64:64 + COMP, r, :], acc[r][64:64 + COMP, :], ACT.Identity).then_inc(z_sb[r], 1)
                sc.wait_ge(z_sb[0], m1 + 1)
                sc.wait_ge(z_sb[1], m1 + 1)
                for part in range(2):
                    sc.dma_start(zv[pair, s, part], zs[64 * part:64 * part + COMP].rearrange(
                        "k g (r c) -> k (g r) c", r=4)).then_inc(z_out, 16)

            sc.sem_inc(z_out, 32)
            sc.sem_inc(z_sb[0], 1)
            sc.sem_inc(z_sb[1], 1)
            with sc.Fori(0, PAIRS) as pair:
                n0 = sc.snap(pair * STRIPS + 1)
                attention(n0)
                transposed(n0)
                attention(sc.snap(n0 + 1))
                token_major(n0)
                transposed(sc.snap(n0 + 1))
                gelu(n0)
                with sc.Fori(0, STRIPS - 2) as s:
                    m1 = sc.snap(n0 + s)
                    n1 = sc.snap(m1 + 2)
                    attention(n1, (pair, s, m1, sc.snap(m1 * 32)))
                    token_major(sc.snap(m1 + 1))
                    transposed(n1)
                    gelu(sc.snap(m1 + 1))
                last = sc.snap(n0 + (STRIPS - 1))
                before = sc.snap(last - 1)
                components(pair, STRIPS - 2, before, sc.snap(before * 32))
                token_major(last)
                gelu(last)
                components(pair, STRIPS - 1, last, sc.snap(last * 32))
            sc.wait_ge(z_out, 32 * (PAIRS * STRIPS + 1))

        @block.vector
        def _(v):
            v.memset(zrow[:], 0.0).then_inc(pads, 1)
            for par in range(2):
                v.memset(xs[par][:, :, :, 0:W + 2:W + 1], 0.0)
                v.memset(xs[par][0:C, :, 0, 1:W + 1], 0.0)
                v.memset(xs[par][C:128, :, 5, 1:W + 1], 0.0).then_inc(pads, 1)
            v.memset(xz[:], 0.0)
            v.memset(probT[:], 0.0).then_inc(pads, 1)
            v.wait_ge(pads, 4)

            def values(n1):
                for j in range(CH):
                    v.wait_ge(v_ps[j], n1)
                    v.tensor_tensor(val[:, j], proj[j % 2][:].rearrange("c (r w) -> c r w", r=4),
                                    val_b[:].unsqueeze(1).to_broadcast([128, 4, 128]), ALU.add).then_inc(v_sb[j], 1)

            def softmax(n1):
                for j in range(CH):
                    scores = scr[j % 2][:].rearrange("c (r w) -> c r w", r=8)
                    v.wait_ge(s_ps[j], n1)
                    v.tensor_reduce(mx[:, j], scores, AX_X, ALU.max).then_inc(s_max[j], 1)
                    v.wait_ge(s_max[j], n1)
                    v.tensor_tensor(prob[:, j], scores, mx[:, j].unsqueeze(2).to_broadcast([128, 8, 64]),
                                    ALU.subtract).then_inc(s_sub[j], 1)
                for j in range(CH):
                    v.wait_ge(s_exp[j], n1)
                    v.tensor_reduce(den[:, j], prob[:, j], AX_X, ALU.add).then_inc(s_sum[j], 1)
                    v.wait_ge(s_sum[j], n1)
                    v.reciprocal(rden[:, j], den[:, j]).then_inc(s_rec[j], 1)

            def with_layer_norm(n1, m1, par):
                statistics(m1)
                residual(n1, par, (0, 1))
                scaled(m1)
                residual(n1, par, (2, 3))
                biased(m1, 0)
                biased(m1, 1)

            def statistics(m1):
                for k in range(TILES // 2):
                    v.wait_ge(f_sb[k], m1)
                    for tl in (2 * k, 2 * k + 1):
                        for a in range(2):
                            st = v.bn_stats(stats[:, tl, a, :], ff[:, tl, a * C:a * C + C])
                st.then_inc(stat_ok, 1)
                v.wait_ge(stat_ok, m1)
                v.tensor_tensor(dmean[:], stats[:, :, :, 1], stats[:, :, :, 4], ALU.subtract).then_inc(dm_ok, 1)
                v.tensor_tensor(msum[:], stats[:, :, :, 2], stats[:, :, :, 5], ALU.add).then_inc(dm_ok, 1)
                v.wait_ge(dm_ok, m1 + m1)
                v.scalar_tensor_tensor(out=dsq[:], in0=dmean[:], scalar=0.25, in1=dmean[:], op0=ALU.mult,
                                       op1=ALU.mult).then_inc(q_ok, 1)
                v.tensor_scalar(msum[:], msum[:], 1.0 / C, LN_EPS, ALU.mult, ALU.add).then_inc(ve_ok, 1)
                v.wait_ge(q_ok, m1)
                v.wait_ge(ve_ok, m1)
                v.tensor_tensor(vare[:], dsq[:], msum[:], ALU.add).then_inc(var_ok, 1)

            def scaled(m1):
                v.wait_ge(rstd_ok, m1)
                v.tensor_tensor(act_h[:].rearrange("p t (a c) -> p (t a) c", a=2),
                                ff[:, :, 128:256].rearrange("p t (a c) -> p t a c", a=2),
                                rstd[:].unsqueeze(3).to_broadcast([128, TILES, 2, C]), ALU.mult).then_inc(hmul, 1)

            def biased(m1, k):
                tl = slice(k * TILES // 2, (k + 1) * TILES // 2)
                v.wait_ge(hmul, m1)
                v.tensor_tensor(act_h[:, tl], act_h[:, tl], ffn_b[:].unsqueeze(1).to_broadcast([128, TILES // 2, 128]),
                                ALU.add).then_inc(hbias[k], 1)

            def residual(n1, par, chunks):
                for j in chunks:
                    v.wait_ge(a_ps[j], n1)
                    at = slice(64 * j, 64 * j + 64)
                    v.tensor_tensor(x1[:, :, at], acc[j % 2][:].rearrange("c (h w) -> c h w", h=WS),
                                    xt[par][:, :, at], ALU.add).then_inc(x1_sb[j], 1)

            def reorder(n1, loads, par):
                v.wait_ge(x_in[par], loads)
                def windows(rows, j):
                    return xt[par][rows, :, 64 * j:64 * j + 64].rearrange("c h (k w) -> c k h w", w=WS)

                for j in range(CH):
                    v.tensor_copy(xw[:, 8 * j:8 * j + 8].rearrange("c k (h w) -> c k h w", w=WS),
                                  windows(slice(0, 128), j)).then_inc(xw_sb[j], 1)
                for j in range(CH):
                    for a in range(2):
                        rows = slice(a * C, a * C + C)
                        last = v.tensor_copy(xz[rows, 8 * j:8 * j + 8, a].rearrange("c k (h w) -> c k h w", w=WS),
                                             windows(rows, j))
                    last.then_inc(xz_sb[j], 1)

            def attention(n1, loads, par):
                reorder(n1, loads, par)
                values(n1)
                softmax(n1)

            for j in range(CH):
                v.sem_inc(x1_sb[j], 2)
            with v.Fori(0, PAIRS) as pair:
                n0 = v.snap(pair * STRIPS + 1)
                v.tensor_copy(val_w[:], val_w_all[:, bass.ds(pair, 1), :].rearrange("c o w -> c (o w)"))
                v.tensor_copy(val_b[:], val_b_all[:, bass.ds(pair, 1), :].rearrange("c o w -> c (o w)"))\
                    .then_inc(pair_w, 1)
                v.wait_ge(pair_w, pair + 1)
                u0 = v.snap(pair * (IN * STRIPS // 2) + IN)
                attention(n0, u0, 0)
                residual(n0, 0, range(CH))
                with v.Fori(0, STRIPS // 2 - 1) as i:
                    for j in range(2):
                        n1 = v.snap(n0 + i * 2 + (1 + j))
                        attention(n1, v.snap(u0 + i * IN + IN * j), (1 + j) % 2)
                        with_layer_norm(n1, v.snap(n1 - 1), (1 + j) % 2)
                last = v.snap(n0 + (STRIPS - 1))
                attention(last, v.snap(u0 + IN * (STRIPS // 2 - 1)), 1)
                with_layer_norm(last, v.snap(last - 1), 1)
                statistics(last)
                scaled(last)
                biased(last, 0)
                biased(last, 1)

        @block.tensor
        def _(p):
            def mm(o, l, r, start=True, stop=True):
                return p.matmul(o, l, r, start=start, stop=stop, skip_group_check=True)

            def project(n1):
                for j in range(CH):
                    if j >= 2:
                        p.wait_ge(g_sb[j - 2], n1)
                    p.wait_ge(xw_sb[j], n1)
                    mm(proj[j % 2][:], g_w[:], xw[:, 8 * j:8 * j + 8].rearrange("c k w -> c (k w)")).then_inc(g_ps[j], 1)
                for j in range(CH):
                    if j < 2:
                        p.wait_ge(g_sb[j + 2], n1)
                    else:
                        p.wait_ge(v_sb[j - 2], n1)
                    p.sem_inc(waited, 1)
                    for m in range(2):
                        for odd in range(2):
                            for up in range(2):
                                k = 2 * m + odd
                                last = mm(proj[j % 2][64 * up:64 * up + 64, 128 * k:128 * k + 128],
                                          xw[:, 8 * j + 4 * m + 2 * up + odd], val_w[:])
                    last.then_inc(v_ps[j], 1)

            def convolve(n1, par, q):
                for pr in range(2):
                    for dx in range(3):
                        for odd in range(2):
                            for a in range(2):
                                k = odd + pr
                                o = 64 * odd + 32 * a
                                last = mm(wide[q][o:o + HID, :], conv_w[:, odd, pr, dx, :],
                                          xs[par][:, a, k:k + 4, dx + q * HALF:dx + q * HALF + HALF],
                                          pr == 0 and dx == 0, pr == 1 and dx == 2)
                last.then_inc(c_ps[q], 1)

            def scores(n1):
                for j in range(CH):
                    p.wait_ge(g_sb[j], n1)
                    p.wait_ge(xz_sb[j], n1)
                    if j >= 2:
                        p.wait_ge(s_sub[j - 2], n1)
                    p.sem_inc(waited, 1)
                    for k in range(4):
                        for odd in range(2):
                            w = 8 * j + 2 * k + odd
                            last = mm(scr[j % 2][64 * odd:64 * odd + 64].rearrange(
                                "q (a k s) -> q a k s", a=2, k=4)[:, :, k, :], g[:, w], xz[:, w])
                    last.then_inc(s_ps[j], 1)

            def transposes(n1):
                for j in range(CH):
                    p.wait_ge(s_nrm[j], n1)
                    if j < 2:
                        p.wait_ge(v_sb[j + 2], n1)
                    else:
                        p.wait_ge(t_sb[j - 2], n1)
                    for k in range(4):
                        last = p.transpose(proj[j % 2][:, 128 * k:128 * k + 128],
                                           prob[:, j, 2 * k:2 * k + 2, :].rearrange("c k s -> c (k s)"), ident[:])
                    last.then_inc(t_ps[j], 1)

            def combine(n1, z1):
                for j in range(CH):
                    if j == 0:
                        p.wait_ge(c_sb[0], n1)
                        p.wait_ge(c_sb[1], n1)
                    if j < 2 and z1 is not None:
                        p.wait_ge(z_sb[j], z1)
                    if j >= 2:
                        p.wait_ge(x1_sb[j - 2], n1 + 2)
                    bank = acc[j % 2][:].rearrange("c (h w) -> c h w", h=WS)
                    for par in range(2):
                        mm(bank[:, par:WS:2], ms2_w[:, par, :], hid[:, j // 2, :, 64 * (j % 2):64 * (j % 2) + 64],
                           par == 0, False)
                    p.wait_ge(t_sb[j], n1)
                    p.sem_inc(waited, 1)
                    for m in range(2):
                        for odd in range(2):
                            for a in range(2):
                                c = slice(a * C, a * C + C)
                                o = acc[j % 2][c].rearrange("c (h m u o w) -> c m o u h w", h=WS, m=2, u=2, o=2)
                                last = mm(o[:, m, odd], val[:, j, 2 * m + odd, c], probT[:, j, 2 * a + m, odd, :],
                                          False, m == 1 and odd == 1)
                    last.then_inc(a_ps[j], 1)

            def token_major(m1, n1):
                for k in range(TILES // 2):
                    if k == 0:
                        for j in range(CH):
                            p.wait_ge(x1_sb[j], m1 + 2)
                    if k < 2:
                        p.wait_ge(s_sub[k + 2], n1)
                    else:
                        p.wait_ge(f_sb[k - 2], m1)
                    for e in range(2):
                        p.transpose(scr[k % 2][:, 256 * e:256 * e + 128], x1[:, k, e * HALF:e * HALF + HALF], ident[:])
                    for e in range(2):
                        for up in range(2):
                            q = slice(64 * up, 64 * up + 64)
                            last = mm(scr[k % 2][q, 256 * e + 128:256 * e + 256],
                                      x1[:, k, e * HALF + 64 * up:e * HALF + 64 * up + 64], ffn_w[:])
                    last.then_inc(f_ps[k], 1)

            def components(m1, x1):
                p.wait_ge(hact, m1)
                for r in range(2):
                    p.wait_ge(x1_sb[2 + r], x1)
                    for e in range(2):
                        tl = slice(8 * r + e, 8 * r + 8, 2)
                        mm(acc[r][0:COMP, :], colb[:, e, :], ff[:, tl, 0:128], e == 0, e == 1)
                        last = mm(acc[r][64:64 + COMP, :], colb[:, e, :], act_h[:, tl, :], e == 0, e == 1)
                    last.then_inc(z_ps[r], 1)

            def attention(n1, loads, par, m1=None):
                p.wait_ge(x_in[par], loads)
                convolve(n1, par, 0)
                if m1 is not None:
                    components(m1, n1 + 1)
                project(n1)
                scores(n1)
                convolve(n1, par, 1)

            def finish(n1, z1=None):
                transposes(n1)
                combine(n1, z1)

            p.wait_ge(consts_in, 16)
            p.wait_ge(pads, 4)
            with p.Fori(0, PAIRS) as pair:
                n0 = p.snap(pair * STRIPS + 1)
                u0 = p.snap(pair * (IN * STRIPS // 2) + IN)
                p.wait_ge(pair_w, pair + 1)
                attention(n0, u0, 0)
                finish(n0, n0)
                second = p.snap(n0 + 1)
                attention(second, u0, 1)
                token_major(n0, second)
                finish(second)
                with p.Fori(0, STRIPS // 2 - 1) as i:
                    for j in range(2):
                        m1 = p.snap(n0 + i * 2 + j)
                        n1 = p.snap(m1 + 2)
                        attention(n1, p.snap(u0 + i * IN + IN), j, m1)
                        token_major(p.snap(m1 + 1), n1)
                        finish(n1, m1 + 1)
                last = p.snap(n0 + (STRIPS - 1))
                components(p.snap(last - 1), last + 2)
                token_major(last, last)
                p.wait_ge(z_sb[0], last)
                p.wait_ge(z_sb[1], last)
                components(last, last + 2)


def modes_and_output(nc, t, comps, out, blur_b, keep):
    with ExitStack() as ctx:
        def sb(name, shape):
            return ctx.enter_context(nc.sbuf_tensor(name, shape, F32))

        def sem(name):
            return ctx.enter_context(nc.semaphore(name))

        fc2_w, same_w, fc2_b = keep["fc2_w"], keep["same_w"], keep["fc2_b"]
        w1 = t["w1"]
        rowb = sb("rowb", [128, 2, M, 2, M])
        xx = sb("xx", [128, M, M, B])
        banks = [ctx.enter_context(nc.psum_tensor(f"tb{i}", [128, BANK], F32)) for i in range(8)]

        consts = sem("tail_consts")
        with ExitStack() as c2:
            comp_in = [c2.enter_context(nc.sbuf_tensor(f"comp_in{i}", [128, COMP, 2, 128], F32)) for i in range(2)]
            dsb = c2.enter_context(nc.sbuf_tensor("dsb", [128, 2, MM], F32))
            loaded = [c2.enter_context(nc.semaphore(f"loaded{i}")) for i in range(2)]
            d_ps, d_sb, u_ps, u_sb = (c2.enter_context(nc.semaphore(n)) for n in ("d_ps", "d_sb", "u_ps", "u_sb"))
            block = c2.enter_context(nc.Block())

            @block.sync
            def _(sp):
                sp.dma_start(rowb[:].rearrange("p a b c d -> p (a b c d)"), t["k_rowb"]).then_inc(consts, 16)
                with sp.Fori(0, PAIRS) as pair:
                    sp.wait_ge(d_ps, pair + 1)
                    for half in range(2):
                        sp.dma_start(comp_in[half][:], comps[pair, half * 128:half * 128 + 128])\
                            .then_inc(loaded[half], 16)

            @block.tensor
            def _(p):
                p.sem_inc(d_ps, 1)
                p.wait_ge(consts, 16)
                with p.Fori(0, PAIRS) as pair:
                    n1 = p.snap(pair + 1)
                    p.wait_ge(d_sb, n1)
                    for half in range(2):
                        p.wait_ge(loaded[half], n1 * 16)
                        for part in range(2):
                            for k2 in range(M):
                                for cs in range(2):
                                    last = p.matmul(banks[part][:, k2 * M:k2 * M + M],
                                                    comp_in[half][:, cs * M + k2, part, :], rowb[:, half, k2, cs, :],
                                                    start=half == 0 and k2 == 0 and cs == 0,
                                                    stop=half == 1 and k2 == M - 1 and cs == 1, skip_group_check=True)
                    last.then_inc(d_ps, 1)
                    p.wait_ge(d_sb, n1 + 1)
                    p.wait_ge(u_sb, n1)
                    for a in range(2):
                        p.matmul(banks[2 + a][:, 0:MM], fc2_w[:, a, :], dsb[:, 1, :], start=True, stop=False,
                                 skip_group_check=True)
                        last = p.matmul(banks[2 + a][:, 0:MM], same_w[:, a, :], dsb[:, 0, :], start=False, stop=True,
                                        skip_group_check=True)
                    last.then_inc(u_ps, 1)

            @block.vector
            def _(v):
                v.sem_inc(d_sb, 1)
                v.sem_inc(u_sb, 1)
                with v.Fori(0, PAIRS) as pair:
                    n1 = v.snap(pair + 1)
                    v.wait_ge(d_ps, n1 + 1)
                    for part in range(2):
                        last = v.tensor_copy(dsb[:, part, :].rearrange("c (i j) -> c i j", i=M),
                                             banks[part][:, 0:MM].rearrange("c (j i) -> c i j", i=M))
                    last.then_inc(d_sb, 1)
                    v.wait_ge(u_ps, n1)
                    for a in range(2):
                        at = v.snap(pair * 2 + a)
                        src = banks[2 + a][:, 0:MM].rearrange("c (i j) -> c i j", i=M)
                        dst = xx[:, :, :, bass.ds(at, 1)].rearrange("c i j o -> c i (j o)")
                        v.tensor_copy(dst[0:C], src[0:C])
                        for di, si in ((slice(0, 1), slice(0, 1)), (slice(1, M), slice(M - 1, 0, -1))):
                            for dj, sj in ((slice(0, 1), slice(0, 1)), (slice(1, M), slice(M - 1, 0, -1))):
                                last = v.tensor_copy(dst[C:128, di, dj], src[C:128, si, sj])
                    last.then_inc(u_sb, 1)

        P2 = M + 2
        ypad = sb("ypad", [C, B, P2, P2])
        yblur = sb("yblur", [C, B, P2, P2])

        with ExitStack() as c2:
            def sb2(name, shape):
                return c2.enter_context(nc.sbuf_tensor(name, shape, F32))

            def sem2(name):
                return c2.enter_context(nc.semaphore(name))

            wa = [sb2(f"wa{i}", [128, C, M]) for i in range(2)]
            wn = [sb2(f"wn{i}", [128, C, M]) for i in range(2)]
            wm = [sb2(f"wm{i}", [128, C, M]) for i in range(2)]
            sign = sb2("sign", [128, 1])
            w_in = [sem2(f"w_in{i}") for i in range(2)]
            w_ok, m_ps, m_sb = sem2("w_ok"), sem2("m_ps"), sem2("m_sb")
            setup, bias_ok, blur_pass = sem2("setup"), sem2("bias_ok"), sem2("blur_pass")
            block = c2.enter_context(nc.Block())

            @block.sync
            def _(sp):
                for i in range(M):
                    if i >= 2:
                        sp.wait_ge(w_ok, i - 1)
                    for lo in (0, C):
                        sp.dma_start(wa[i % 2][lo:lo + C], w1[:, :, i, :]).then_inc(w_in[i % 2], 16)
                        sp.dma_start(wn[i % 2][lo:lo + C], w1[:, :, (M - i) % M, :]).then_inc(w_in[i % 2], 16)

            @block.vector
            def _(v):
                def mixed(i):
                    v.wait_ge(m_ps, i + 1)
                    v.tensor_copy(ypad[:, :, i + 1, 1:M + 1],
                                  banks[i % 4][0:C, 0:M * B].rearrange("c (j b) -> c b j", b=B)).then_inc(m_sb, 1)

                v.memset(sign[0:C], 1.0)
                v.memset(sign[C:128], -1.0)
                v.memset(ypad[:], 0.0).then_inc(setup, 1)
                v.wait_ge(setup, 1)
                v.tensor_scalar(xx[:, 0, 0, :], xx[:, 0, 0, :], fc2_b[:], None, ALU.add).then_inc(bias_ok, 1)
                for i in range(M):
                    k = i % 2
                    v.wait_ge(w_in[k], 64 * (i // 2 + 1))
                    if i >= 2:
                        v.wait_ge(m_ps, i - 1)
                    v.scalar_tensor_tensor(out=wm[k][:, :, 0:1], in0=wn[k][:, :, 0:1], scalar=sign[:],
                                           in1=wa[k][:, :, 0:1], op0=ALU.mult, op1=ALU.add)
                    v.scalar_tensor_tensor(out=wm[k][:, :, 1:M], in0=wn[k][:, :, M - 1:0:-1], scalar=sign[:],
                                           in1=wa[k][:, :, 1:M], op0=ALU.mult, op1=ALU.add).then_inc(w_ok, 1)
                    if i >= 1:
                        mixed(i - 1)
                mixed(M - 1)
                v.wait_ge(m_sb, M)
                for s in range(B):
                    if s:
                        v.wait_ge(blur_pass, s)
                    for b in range(B):
                        src, dst = ypad[:, s].rearrange("c i j -> c (i j)"), yblur[:, b].rearrange("c i j -> c (i j)")
                        if s == 0:
                            last = v.tensor_scalar(dst, src, float(blur_b[b, s]), None, ALU.mult)
                        elif blur_b[b, s] != 0.0:
                            last = v.scalar_tensor_tensor(out=dst, in0=src, scalar=float(blur_b[b, s]), in1=dst,
                                                          op0=ALU.mult, op1=ALU.add)
                    last.then_inc(blur_pass, 1)

            @block.tensor
            def _(p):
                p.wait_ge(bias_ok, 1)
                for i in range(M):
                    p.wait_ge(w_ok, i + 1)
                    if i >= 4:
                        p.wait_ge(m_sb, i - 3)
                    for j in range(M):
                        last = p.matmul(banks[i % 4][0:C, j * B:j * B + B], wm[i % 2][:, :, j], xx[:, i, j, :],
                                        start=True, stop=True)
                    last.then_inc(m_ps, 1)

        with ExitStack() as c2:
            def sb2(name, shape):
                return c2.enter_context(nc.sbuf_tensor(name, shape, F32))

            def sem2(name):
                return c2.enter_context(nc.semaphore(name))

            def sems2(name, n):
                return [sem2(f"{name}{i}") for i in range(n)]

            GO = 4
            GROUPS = C // GO
            DEEP = 4
            ycur = sb2("ycur", [C, P2, P2])
            blurc = sb2("blurc", [C, C])
            inv = sb2("inv", [128, H])
            invc = sb2("invc", [64, 2, KEPT])
            tcur = sb2("tcur", [64, 32, C])
            rr = [sb2(f"rr{i}", [128, 2 * KEPT]) for i in range(2)]
            stage = [[sb2(f"stage{i}_{hh}", [128, GO, W]) for hh in range(2)] for i in range(DEEP)]
            tail_in, clear = sem2("tail_in"), sem2("clear")
            waited = sem2("waited_tail")
            y_sb, t_ps, t_sb = sem2("y_sb"), sem2("t_ps"), sem2("t_sb")
            r_ps, r_sb = sem2("r_ps"), sem2("r_sb")
            o_ps = sems2("o_ps", 2)
            o_sb = sems2("o_sb", 2)
            stored = [sems2(f"stored{hh}_", DEEP) for hh in range(2)]
            block = c2.enter_context(nc.Block())

            def evacuate(eng, copy, b, n16, g, hh):
                slot = g % DEEP
                eng.wait_ge(o_ps[hh], n16 + g)
                eng.wait_ge(stored[hh][slot], (b * (GROUPS // DEEP) + (g // DEEP + 1)) * 16)
                for oo in range(2):
                    src = banks[4 + 2 * hh + oo][:, 0:2 * KEPT].rearrange("h (o w) -> h o w", w=KEPT)
                    copy(stage[slot][hh][:, oo:GO:2, 0:KEPT_LO], src[:, :, 0:KEPT_LO])
                    last = copy(stage[slot][hh][:, oo:GO:2, W - KEPT_HI:W], src[:, :, KEPT_LO:KEPT])
                last.then_inc(o_sb[hh], 1)

            @block.sync
            def _(sp):
                for dst, src in ((blurc[:], t["k_blurc"]), (inv[:], t["k_inv"]), (invc[:], t["k_invc"])):
                    sp.dma_start(dst, src).then_inc(tail_in, 16)
                with sp.Fori(0, B) as b:
                    n16 = sp.snap(b * GROUPS + 2)
                    for g in range(GROUPS):
                        for hh in range(2):
                            sp.wait_ge(o_sb[hh], n16 + g)
                            sp.dma_start(out[b, g * GO:g * GO + GO, hh * 128:hh * 128 + 128, :]
                                         .rearrange("o h w -> h o w"), stage[g % DEEP][hh][:])\
                                .then_inc(stored[hh][g % DEEP], 16)
                for hh in range(2):
                    for slot in range(DEEP):
                        sp.wait_ge(stored[hh][slot], 16 * (B * GROUPS // DEEP + 1))

            @block.vector
            def _(v):
                v.memset(tcur[:], 0.0)
                for slot in range(DEEP):
                    for hh in range(2):
                        last = v.memset(stage[slot][hh][:], 0.0)
                last.then_inc(clear, 1)
                v.sem_inc(o_sb[1], 1)
                for slot in range(DEEP):
                    v.sem_inc(stored[1][slot], 16)
                v.wait_ge(clear, 1)
                with v.Fori(0, B) as b:
                    n1 = v.snap(b + 1)
                    n16 = v.snap(b * GROUPS + 1)
                    v.tensor_copy(ycur[:], yblur[:, bass.ds(b, 1)].rearrange("c o i j -> c (o i) j")).then_inc(y_sb, 1)
                    for c in range(3):
                        v.wait_ge(t_ps, b * 3 + (c + 1))
                        for q in (0, 32):
                            last = v.tensor_copy(tcur[q:q + M1, 7 * c:7 * c + 7, :],
                                                 banks[c % 2][q:q + M1, 0:7 * C].rearrange("q (m o) -> q m o", o=C))
                        last.then_inc(t_sb, 1)
                    for g in range(GROUPS):
                        evacuate(v, v.tensor_copy, b, n16, g, 1)

            @block.scalar
            def _(sc):
                def copy(dst, src):
                    return sc.activation(dst, src, ACT.Identity)

                sc.sem_inc(o_sb[0], 1)
                for slot in range(DEEP):
                    sc.sem_inc(stored[0][slot], 16)
                sc.wait_ge(clear, 1)
                with sc.Fori(0, B) as b:
                    n16 = sc.snap(b * GROUPS + 1)
                    for g in range(GROUPS + 1):
                        if g < GROUPS:
                            sc.wait_ge(r_ps, n16 + g)
                            copy(rr[g % 2][:], banks[2 + g % 2][:, 0:2 * KEPT]).then_inc(r_sb, 1)
                        if g >= 1:
                            evacuate(sc, copy, b, n16, g - 1, 0)

            @block.tensor
            def _(p):
                p.wait_ge(tail_in, 48)
                p.wait_ge(clear, 1)
                with p.Fori(0, B) as b:
                    n1 = p.snap(b + 1)
                    n16 = p.snap(b * GROUPS + 1)
                    p.wait_ge(y_sb, n1)
                    p.sem_inc(waited, 1)
                    for c in range(3):
                        if c == 2:
                            p.wait_ge(t_sb, b * 3 + 1)
                            p.sem_inc(waited, 1)
                        for m in range(7 * c, 7 * c + 7):
                            for q, y in ((0, ycur[:, m + 1, 1:1 + M1]), (32, ycur[:, m, 0:M1])):
                                last = p.matmul(banks[c % 2][q:q + M1, (m - 7 * c) * C:(m - 7 * c) * C + C], y,
                                                blurc[:], start=True, stop=True)
                        last.then_inc(t_ps, 1)
                    p.wait_ge(t_sb, b * 3 + 3)
                    p.sem_inc(waited, 1)
                    for g in range(GROUPS + 1):
                        if g < GROUPS:
                            for c in range(2):
                                for oo in range(2):
                                    for cs in range(2):
                                        q = 64 * oo + 32 * cs
                                        last = p.matmul(banks[2 + g % 2][q:q + 32, c * KEPT:c * KEPT + KEPT],
                                                        tcur[:, :, g * GO + 2 * c + oo], invc[:, cs, :],
                                                        start=True, stop=True, tile_position=(0, q))
                            last.then_inc(r_ps, 1)
                        if g >= 1:
                            k = g - 1
                            p.wait_ge(r_sb, n16 + k)
                            for hh in range(2):
                                p.wait_ge(o_sb[hh], n16 + k)
                                for oo in range(2):
                                    s = slice(64 * oo, 64 * oo + 64)
                                    last = p.matmul(banks[4 + 2 * hh + oo][:, 0:2 * KEPT],
                                                    inv[s, hh * 128:hh * 128 + 128], rr[k % 2][s, :],
                                                    start=True, stop=True)
                                last.then_inc(o_ps[hh], 1)


_LAYER0 = ["qk_w", "qk_b", "v_w", "v_b", "out_w", "out_b", "ms1_w", "ms1_b", "ms2_w", "ms2_b", "se1_w", "se1_b",
           "se2_w", "se2_b", "ln_g", "ln_b", "fc1_w", "fc1_b", "fc2_w", "fc2_b"]


def kernel(**inputs):
    import concourse.bacc as _bacc
    from concourse.bass_utils import run_bass_kernel_spmd as _run

    nc = _bacc.Bacc("TRN2", target_bir_lowering=False, num_devices=1)
    arrays, tensors = {}, {}
    given = {"x": inputs["x"], "w1": inputs["L1_conv_w1"]}
    given.update({name: inputs["L0_conv_" + name] for name in _LAYER0})
    tables = {name: a.astype(np.float32) for name, a in shape_constants().items()}
    for name, a in list(given.items()) + list(tables.items()):
        a = np.ascontiguousarray(a)
        arrays[f"in_{name}"] = a
        tensors[name] = nc.dram_tensor(f"in_{name}", a.shape, F32, kind="ExternalInput").ap()
    out = nc.dram_tensor("out_0", (B, C, H, W), F32, kind="ExternalOutput").ap()
    conv_layer_then_hartley_kernel(nc, tensors, out)
    r = _run(nc, [arrays], core_ids=[0])
    return r.results[0]["out_0"]
```

```python
from contextlib import ExitStack

import numpy as np
import concourse.bass as bass
from concourse import mybir

F32 = mybir.dt.float32
ALU = mybir.AluOpType
ACT = mybir.ActivationFunctionType
AX_X = mybir.AxisListType.X

B, C, H, W = 8, 64, 256, 256
PAIRS = B // 2
WS = 8
STRIPS = H // WS
WIN = W // WS
HALF = W // 2
PX = WS * W
HID = C // 2
SE = C // 16
M = 20
MM = M * M
COMP = 2 * M
M1 = M + 1
KEPT_LO, KEPT_HI = 65, 64
KEPT = KEPT_LO + KEPT_HI
SCALE = 1.0 / C ** 0.5
LN_EPS = 1e-5
CH = 4
BANK = 512


RADIUS = 4


def blur_taps(sigma=1.0):
    t = np.arange(-RADIUS, RADIUS + 1, dtype=np.float32)
    k = np.exp(-0.5 * (t / sigma) ** 2)
    return (k / k.sum()).astype(np.float64)


def blur_matrix(n):
    k = blur_taps()
    g = np.zeros((n, n))
    for i in range(n):
        for j in range(2 * RADIUS + 1):
            g[i, min(max(i + j - RADIUS, 0), n - 1)] += k[j]
    return g


def shape_constants():
    two_pi = 2 * np.pi
    ident = np.eye(128)
    ang = two_pi * np.outer(np.arange(W), np.arange(M)) / W
    colb = np.concatenate([np.cos(ang), np.sin(ang)], 1).reshape(2, 128, COMP).transpose(1, 0, 2)
    h = np.arange(H)[:, None, None]
    k2 = np.arange(M)[None, :, None]
    k1 = np.arange(M)[None, None, :]
    a1 = two_pi * h * k1 / H
    phi = two_pi * (k1 + k2) / H
    rowb = np.stack([np.cos(a1) - np.sin(a1 + phi), -np.sin(a1) - np.cos(a1 + phi)], 2)
    rowb = rowb.reshape(2, 128, M, 2, M).transpose(1, 0, 2, 3, 4)
    rowb = np.pad(rowb, [(0, 0)] * 4 + [(0, 32 - M)])
    m = np.arange(M1)
    inv = np.zeros((2, 32, H))
    inv[0, :M1] = np.cos(two_pi * np.outer(m, np.arange(H)) / H)
    inv[1, :M1] = np.sin(two_pi * np.outer(m, np.arange(H)) / H)
    inv = (inv.reshape(64, H) @ blur_matrix(H).T) * (0.5 / (H * W))
    inv2 = np.zeros((128, 2, H))
    inv2[:64, 0], inv2[64:, 1] = inv, inv
    keep = np.r_[0:KEPT_LO, W - KEPT_HI:W]
    c = np.cos(two_pi * np.outer(m, np.arange(W)) / W)
    s = np.sin(two_pi * np.outer(m, np.arange(W)) / W)
    invc = np.zeros((128, 2, W))
    invc[0:M1, 0], invc[32:32 + M1, 0], invc[0:M1, 1], invc[32:32 + M1, 1] = c, -s, -s, -c
    invc = (invc @ blur_matrix(W).T)[:, :, keep]
    center = np.eye(C) - 1.0 / C
    return {
        "k_ident": ident, "k_colb": colb, "k_rowb": rowb.reshape(128, -1), "k_inv": inv2,
        "k_invc": invc, "k_center": np.concatenate([center, center], 1),
        "k_blurc": np.pad(blur_matrix(C).T, [(0, 128 - C), (0, 0)]),
    }


def conv_layer_then_hartley_kernel(nc, t, out):
    x_pair = t["x"].rearrange("(p a) c h w -> p (a c) h w", a=2)
    comps = nc.dram_tensor("mode_columns", [PAIRS, H, COMP, 2, 2 * C], F32, kind="Internal").ap()

    top = ExitStack()
    with top:
        def keep_sb(name, shape):
            return top.enter_context(nc.sbuf_tensor(name, shape, F32))

        ident = keep_sb("ident", [128, 128])
        g_w = keep_sb("g_w", [128, 128])
        g_b = keep_sb("g_b", [128, 1])
        val_w = keep_sb("val_w", [128, 128])
        val_b = keep_sb("val_b", [128, 128])
        sums = keep_sb("sums", [128, STRIPS])
        vw_plain = keep_sb("vw_plain", [128, C])
        obv_row = keep_sb("obv_row", [128, C])
        ms2b_row = keep_sb("ms2b_row", [128, C])
        se1_t = keep_sb("se1_t", [128, SE])
        se1_b = keep_sb("se1_b", [SE, 1])
        se2_t = keep_sb("se2_t", [SE, 2, C])
        se2_b = keep_sb("se2_b", [128, 1])
        conv_w = keep_sb("conv_w", [128, 2, 2, 4, HID])
        conv_b = keep_sb("conv_b", [128, 1])
        ms2_w = keep_sb("ms2_w", [128, 2, 128])
        ffn_w = keep_sb("ffn_w", [128, 128])
        ffn_b = keep_sb("ffn_b", [128, 128])
        fc2_w = keep_sb("fc2_w", [128, 2, 128])
        same_w = keep_sb("same_w", [128, 2, 128])
        fc2_b = keep_sb("fc2_b", [128, 1])

        prepare(nc, t, x_pair, locals())
        main(nc, t, x_pair, comps, locals())
        modes_and_output(nc, t, comps, out, locals())


def prepare(nc, t, x_pair, keep):
    with ExitStack() as ctx:
        def sb(name, shape):
            return ctx.enter_context(nc.sbuf_tensor(name, shape, F32))

        def sem(name):
            return ctx.enter_context(nc.semaphore(name))

        ident, g_w, g_b = keep["ident"], keep["g_w"], keep["g_b"]
        val_w, sums, vw_plain, obv_row, ms2b_row = (
            keep[k] for k in ("val_w", "sums", "vw_plain", "obv_row", "ms2b_row"))
        se1_t, se1_b, se2_t, se2_b = (keep[k] for k in ("se1_t", "se1_b", "se2_t", "se2_b"))
        conv_w, conv_b, ms2_w = keep["conv_w"], keep["conv_b"], keep["ms2_w"]
        ffn_w, ffn_b, fc2_w, same_w, fc2_b = (keep[k] for k in ("ffn_w", "ffn_b", "fc2_w", "same_w", "fc2_b"))

        PIECE = 32
        PIECES = H // PIECE
        xs = sb("xs", [128, 2, PIECE * W])
        junk = sb("junk", [128, PIECE * W])
        wq2 = sb("wq2", [C, 2, C])
        wk2 = sb("wk2", [C, 2, C])
        bq = sb("bq", [C, 1])
        vw2 = sb("vw2", [C, 2, C])
        vb = sb("vb", [C, 1])
        ow_t = sb("ow_t", [C, C])
        ob = sb("ob", [C, 1])
        ms1_raw = sb("ms1_raw", [HID, C * 9])
        conv_t = sb("conv_t", [128, 3, 3, HID])
        outer = sb("outer", [128, 3, HID])
        wino = sb("wino", [128, 3, 4, HID])
        fc1_t = sb("fc1_t", [C, C])
        ln_g = sb("ln_g", [C, 1])
        ln_b = sb("ln_b", [C, 1])
        fc1b_row = sb("fc1b_row", [128, C])
        fc2b_raw = sb("fc2b_raw", [128, 1])
        center = sb("center", [C, 128])
        fc1_g = sb("fc1_g", [C, C])
        ln_b_wide = sb("ln_b_wide", [C, 128])
        obv = sb("obv", [C, 1])
        obv_wide = sb("obv_wide", [C, 128])
        pA = ctx.enter_context(nc.psum_tensor("pA", [128, BANK], F32))
        pB = ctx.enter_context(nc.psum_tensor("pB", [128, BANK], F32))
        pD = ctx.enter_context(nc.psum_tensor("pD", [128, BANK], F32))

        weights_in, zeroed, placed = sem("weights_in"), sem("zeroed"), sem("placed")
        piece_in = [sem("piece_in0"), sem("piece_in1")]
        piece_sum = sem("piece_sum")
        dve, pe = sem("dve_step"), sem("pe_step")

        def vec(name):
            return t[name].rearrange("(c o) -> c o", o=1)

        loads = [
            (ident[:], t["k_ident"]), (center[:], t["k_center"]),
            (bq[:], vec("qk_b")[0:C]), (vb[:], vec("v_b")), (ob[:], vec("out_b")),
            (ms1_raw[:], t["ms1_w"].rearrange("o c kh kw -> o (c kh kw)")),
            (ms2b_row[:], t["ms2_b"].partition_broadcast(128)),
            (fc1b_row[:], t["fc1_b"].partition_broadcast(128)),
            (se1_b[:], vec("se1_b")), (ln_g[:], vec("ln_g")), (ln_b[:], vec("ln_b")),
            (fc1_t[:], t["fc1_w"].rearrange("o c -> c o")),
            (ow_t[:], t["out_w"].rearrange("o c -> c o")),
        ]
        for a in range(2):
            lo, hi = a * C, a * C + C
            loads += [
                (wq2[:, a, :], t["qk_w"][0:C, :]), (wk2[:, a, :], t["qk_w"][C:2 * C, :]),
                (vw2[:, a, :], t["v_w"]), (se2_b[lo:hi, :], vec("se2_b")),
                (se1_t[lo:hi, :], t["se1_w"].rearrange("o c -> c o")),
                (se2_t[:, a, :], t["se2_w"].rearrange("o c -> c o")),
                (fc2b_raw[lo:hi, :], vec("fc2_b")),
            ]
            for par in range(2):
                r = par * C + a * HID
                loads += [(conv_b[r:r + HID, :], vec("ms1_b"))]
        late = []
        for a in range(2):
            for par in range(2):
                r = par * C + a * HID
                late += [(ms2_w[r:r + HID, par, a * C:a * C + C], t["ms2_w"].rearrange("o c -> c o"))]
                late += [(fc2_w[a * C:a * C + C, a, par * C:par * C + C], t["fc2_w"].rearrange("o c -> c o")),
                         (same_w[a * C:a * C + C, a, par * C:par * C + C], t["k_ident"][0:C, 0:C])]

        block = ctx.enter_context(nc.Block())

        @block.sync
        def _(sp):
            for q in range(PIECES):
                if q >= 2:
                    sp.wait_ge(piece_sum, q - 1)
                sp.dma_start(xs[:, q % 2, :], x_pair[0, :, q * PIECE:(q + 1) * PIECE, :].rearrange("c h w -> c (h w)"))\
                    .then_inc(piece_in[q % 2], 16)

        @block.gpsimd
        def _(pool):
            for dst, src in loads:
                pool.dma_start(dst, src, allow_slow_non_contiguous=True).then_inc(weights_in, 16)
            pool.wait_ge(zeroed, 1)
            for dst, src in late:
                pool.dma_start(dst, src, allow_slow_non_contiguous=True).then_inc(placed, 16)
            pool.wait_ge(placed, 16 * len(late))

        @block.scalar
        def _(sc):
            for q in range(PIECES):
                sc.wait_ge(piece_in[q % 2], 16 * (q // 2 + 1))
                if q >= 1:
                    sc.wait_ge(piece_sum, q)
                sc.activation(junk[:], xs[:, q % 2, :], ACT.Copy, accum_out=sums[:, q:q + 1]).then_inc(piece_sum, 1)

        @block.vector
        def _(v):
            steps = [0]

            def link(ins):
                steps[0] += 1
                ins.then_inc(dve, 1)
                v.wait_ge(dve, steps[0])

            for tile in (conv_w, ms2_w, fc2_w, same_w, ffn_w, g_w):
                v.memset(tile[:], 0.0)
            v.memset(sums[:, PIECES:STRIPS], 0.0)
            v.memset(val_w[:], 0.0).then_inc(zeroed, 1)
            v.wait_ge(zeroed, 1)
            v.wait_ge(weights_in, 16 * len(loads))
            link(v.tensor_scalar(fc1_g[:], fc1_t[:], ln_g[:], None, ALU.mult))
            link(v.tensor_copy(ln_b_wide[:], ln_b[:].to_broadcast([C, 128])))
            v.wait_ge(pe, 1)
            for a in range(2):
                s = slice(a * C, a * C + C)
                v.tensor_scalar(g_w[s, s], pA[s, 0:C], SCALE, None, ALU.mult)
            v.tensor_scalar(g_b[:], pA[:, 2 * C:2 * C + 1], SCALE, None, ALU.mult)
            v.tensor_scalar(fc2_b[:], fc2b_raw[:], float(H * W), None, ALU.mult)
            v.wait_ge(pe, 2)
            link(v.tensor_copy(conv_t[:], pB[:, 0:9 * HID].rearrange("c (i j o) -> c i j o", i=3, j=3)))
            link(v.tensor_tensor(outer[:], conv_t[:, :, 0], conv_t[:, :, 2], ALU.add))
            v.tensor_copy(wino[:, :, 0], conv_t[:, :, 0])
            v.tensor_tensor(wino[:, :, 1], outer[:], conv_t[:, :, 1], ALU.add)
            v.tensor_tensor(wino[:, :, 2], outer[:], conv_t[:, :, 1], ALU.subtract)
            link(v.tensor_copy(wino[:, :, 3], conv_t[:, :, 2]))
            link(v.tensor_scalar(wino[:, :, 1:3], wino[:, :, 1:3], 0.5, None, ALU.mult))
            for rp, par, pr, kh in ((1, 0, 0, 0), (0, 0, 1, 1), (1, 0, 1, 2), (0, 1, 0, 0), (1, 1, 0, 1), (0, 1, 1, 2)):
                s = slice(rp * C, rp * C + C)
                v.tensor_copy(conv_w[s, par, pr], wino[s, kh])
            v.wait_ge(pe, 3)
            for a in range(2):
                s = slice(a * C, a * C + C)
                v.tensor_copy(ffn_w[s, s], pD[s, 0:C])
                v.tensor_tensor(ffn_b[:, s], pD[:, C:2 * C], fc1b_row[:], ALU.add)
            v.tensor_copy(vw_plain[:], pD[:, 2 * C:3 * C])
            link(v.tensor_tensor(obv[:], pD[0:C, 3 * C:3 * C + 1], ob[:], ALU.add))
            link(v.tensor_copy(obv_wide[:], obv[:].to_broadcast([C, 128])))
            v.wait_ge(pe, 4)
            v.tensor_copy(obv_row[:], pD[:, 256:256 + C])

        @block.tensor
        def _(p):
            def mm(o, l, r, last=False):
                i = p.matmul(o, l, r, start=True, stop=True)
                if last:
                    i.then_inc(pe, 1)

            p.wait_ge(weights_in, 16 * len(loads))
            mm(pA[:, 0:C], wq2[:].rearrange("o a c -> o (a c)"), wk2[:, 0, :])
            mm(pA[:, 2 * C:2 * C + 1], wk2[:].rearrange("o a c -> o (a c)"), bq[:], True)
            raw = ms1_raw[:].rearrange("o (c k) -> o k c", k=9)
            for k in range(9):
                for a in range(2):
                    mm(pB[a * C:a * C + C, k * HID:k * HID + HID], raw[:, k, :], ident[0:HID, 0:HID], k == 8 and a == 1)
            p.wait_ge(dve, 2)
            mm(pD[:, 0:C], center[:], fc1_g[:])
            mm(pD[:, C:2 * C], ln_b_wide[:], fc1_t[:])
            mm(pD[:, 2 * C:3 * C], vw2[:].rearrange("o a c -> o (a c)"), ow_t[:])
            mm(pD[0:C, 3 * C:3 * C + 1], ow_t[:], vb[:], True)
            p.wait_ge(dve, 8)
            mm(pD[:, 256:256 + C], obv_wide[:], ident[0:C, 0:C], True)

def main(nc, t, x_pair, comps, keep):
    with ExitStack() as ctx:
        def sb(name, shape):
            return ctx.enter_context(nc.sbuf_tensor(name, shape, F32))

        def ps(name):
            return ctx.enter_context(nc.psum_tensor(name, [128, BANK], F32))

        def sem(name):
            return ctx.enter_context(nc.semaphore(name))

        def sems(name, n):
            return [sem(f"{name}{i}") for i in range(n)]

        g_w, g_b, conv_w, conv_b, ms2_w = (keep[k] for k in ("g_w", "g_b", "conv_w", "conv_b", "ms2_w"))
        ffn_w, ffn_b, ident = keep["ffn_w"], keep["ffn_b"], keep["ident"]
        val_w, val_b, sums, vw_plain, obv_row, ms2b_row = (
            keep[k] for k in ("val_w", "val_b", "sums", "vw_plain", "obv_row", "ms2b_row"))
        se1_t, se1_b, se2_t, se2_b = (keep[k] for k in ("se1_t", "se1_b", "se2_t", "se2_b"))

        IN = 7 * 16
        TILES = PX // 128
        xt = [sb(f"xt{i}", [128, WS, W]) for i in range(2)]
        xs = [sb(f"xs{i}", [128, 2, WS // 2 + 2, W + 2]) for i in range(2)]
        zrow = sb("zrow", [128, 2, W])
        cin = sb("cin", [128, 2, 4, 2, WS // 2 + 2, HALF // 2])
        msum12 = sb("msum12", [128, 2, PX // 8])
        mdif12 = sb("mdif12", [128, 2, PX // 8])
        cout = sb("cout", [128, 2, PX // 8, 2])
        xg = sb("xg", [128, PX])
        gap = sb("gap", [128, 1])
        hidden = sb("hidden", [SE, 2])
        gate = sb("gate", [128, 2])
        gate_wide = sb("gate_wide", [C, 2, 128])
        gate_row = sb("gate_row", [128, 2, C])
        g = sb("g", [128, WIN, WS * WS])
        xw = sb("xw", [128, WIN, WS * WS])
        xz = sb("xz", [128, WIN, 2, WS * WS])
        val = sb("val", [128, CH, 4, 128])
        prob = sb("prob", [128, CH, 8, 64])
        probT = sb("probT", [128, CH, 4, 2, 128])
        mx = sb("mx", [128, CH, 8])
        den = sb("den", [128, CH, 8])
        rden = sb("rden", [128, CH, 8])
        hid = sb("hid", [128, 2, 4, HALF])
        x1 = sb("x1", [128, WS, W])
        ff = sb("ff", [128, TILES, 256])
        act_h = sb("act_h", [128, TILES, 128])
        stats = sb("stats", [128, TILES, 2, 6])
        dmean = sb("dmean", [128, TILES, 2])
        msum = sb("msum", [128, TILES, 2])
        dsq = sb("dsq", [128, TILES, 2])
        vare = sb("vare", [128, TILES, 2])
        rstd = sb("rstd", [128, TILES, 2])
        minus_half = sb("minus_half", [128, TILES, 2])
        colb = sb("colb", [128, 2, COMP])
        zs = sb("zs", [128, 2, BANK])
        proj = [ps("proj0"), ps("proj1")]
        wide = [ps("wide0"), ps("wide1")]
        acc = [ps("acc0"), ps("acc1")]
        scr = [ps("scr0"), ps("scr1")]
        token_banks = proj + scr

        x_in = sems("x_in", 2)
        consts_in, pads = sem("consts_in"), sem("pads")
        waited = sem("waited")
        xg_in, sum_ok = sem("xg_in"), sem("sum_ok")
        gate_dve, gate_pe, gate_act = sem("gate_dve"), sem("gate_pe"), sem("gate_act")
        pair_w = sem("pair_w")
        xw_sb, xz_sb = sems("xw_sb", CH), sems("xz_sb", CH)
        g_ps, g_sb = sems("g_ps", CH), sems("g_sb", CH)
        v_ps, v_sb = sems("v_ps", CH), sems("v_sb", CH)
        c_in, c_ps = sems("c_in", 2), sems("c_ps", 2)
        c_half = sems("c_half", 2)
        c_out, c_sb = sems("c_out", 2), sems("c_sb", 2)
        s_ps, s_max, s_sub = sems("s_ps", CH), sems("s_max", CH), sems("s_sub", CH)
        s_exp, s_sum, s_rec, s_nrm = sems("s_exp", CH), sems("s_sum", CH), sems("s_rec", CH), sems("s_nrm", CH)
        t_ps, t_sb = sems("t_ps", CH), sems("t_sb", CH)
        a_ps, x1_sb = sems("a_ps", CH), sems("x1_sb", CH)
        f_ps, f_sb = sem("f_ps"), sem("f_sb")
        stat_ok, dm_ok, q_ok, ve_ok, var_ok = sem("stat_ok"), sem("dm_ok"), sem("q_ok"), sem("ve_ok"), sem("var_ok")
        rstd_ok = sem("rstd_ok")
        hmul, hbias, hact = sem("hmul"), sems("hbias", 2), sem("hact")
        z_ps, z_sb = sems("z_ps", 2), sems("z_sb", 2)
        z_out = sem("z_out")

        x_rows = t["x"].rearrange("b c (k r) w -> b r c k w", r=2)
        x_images = t["x"].rearrange("(p a) c h w -> p c a h w", a=2)
        zv = comps.rearrange("p (s r) k m c -> p s m k r c", r=WS)

        block = ctx.enter_context(nc.Block())

        @block.sync
        def _(sp):
            sp.dma_start(colb[:], t["k_colb"]).then_inc(consts_in, 16)
            sp.wait_ge(pads, 4)

            def load(pair, s, n1, par, first=False, last=False):
                sp.wait_ge(x1_sb[CH - 1], n1)
                r0 = s * WS
                sp.dma_start(xt[par][:], x_pair[pair, :, bass.ds(r0, WS), :]).then_inc(x_in[par], 16)
                for a in range(2):
                    own = x_rows[pair * 2 + a]
                    sp.dma_start(xs[par][0:C, a, 1:5, 1:W + 1], own[0, :, bass.ds(s * 4, 4), :])\
                        .then_inc(x_in[par], 16)
                    sp.dma_start(xs[par][C:128, a, 1:5, 1:W + 1], own[1, :, bass.ds(s * 4, 4), :])\
                        .then_inc(x_in[par], 16)
                above, below = xs[par][C:128, :, 0, 1:W + 1], xs[par][0:C, :, 5, 1:W + 1]
                if first:
                    sp.dma_start(above, zrow[C:128]).then_inc(x_in[par], 16)
                else:
                    sp.dma_start(above, x_images[pair, :, :, bass.ds(r0 - 1, 1), :].rearrange("c a h w -> c a (h w)"))\
                        .then_inc(x_in[par], 16)
                if last:
                    sp.dma_start(below, zrow[0:C]).then_inc(x_in[par], 16)
                else:
                    sp.dma_start(below, x_images[pair, :, :, bass.ds(r0 + WS, 1), :].rearrange("c a h w -> c a (h w)"))\
                        .then_inc(x_in[par], 16)

            with sp.Fori(0, PAIRS) as pair:
                n0 = sp.snap(pair * STRIPS + 1)
                load(pair, 0, n0, 0, first=True)
                with sp.Fori(0, STRIPS // 2 - 1) as i:
                    for j in range(2):
                        s = sp.snap(i * 2 + (1 + j))
                        load(pair, s, sp.snap(n0 + s), (1 + j) % 2)
                load(pair, STRIPS - 1, sp.snap(n0 + (STRIPS - 1)), 1, last=True)

        @block.gpsimd
        def _(pool):
            pool.memset(minus_half[:], -0.5)

            def conv_inputs(n1, loads, par, q, products=(0, 1, 2, 3)):
                if products[0] == 0:
                    pool.wait_ge(x_in[par], loads)
                    pool.wait_ge(c_ps[q], n1)
                d = [xs[par][:, :, :, q * HALF + k:q * HALF + k + HALF - 1:2].rearrange("c a r t -> c (a r) t")
                     for k in range(4)]
                for k in products:
                    one, other, op = ((0, 2, ALU.subtract), (1, 2, ALU.add), (2, 1, ALU.subtract),
                                      (1, 3, ALU.subtract))[k]
                    last = pool.tensor_tensor(cin[:, q, k].rearrange("c a r t -> c (a r) t"), d[one], d[other], op)
                if products[-1] == 3:
                    last.then_inc(c_in[q], 1)

            def attention(n1):
                for j in range(CH):
                    pool.wait_ge(s_rec[j], n1)
                    pool.tensor_tensor(prob[:, j], prob[:, j], rden[:, j].unsqueeze(2).to_broadcast([128, 8, 64]),
                                       ALU.mult).then_inc(s_nrm[j], 1)

            def feed_forward(m1):
                pool.wait_ge(var_ok, m1)
                pool.tensor_tensor(rstd[:], vare[:], minus_half[:], ALU.pow).then_inc(rstd_ok, 1)

            with pool.Fori(0, PAIRS) as pair:
                n0 = pool.snap(pair * STRIPS + 1)
                u0 = pool.snap(pair * (IN * STRIPS // 2) + IN)
                conv_inputs(n0, u0, 0, 0)
                conv_inputs(n0, u0, 0, 1)
                second = pool.snap(n0 + 1)
                conv_inputs(second, u0, 1, 0)
                attention(n0)
                conv_inputs(second, u0, 1, 1)
                with pool.Fori(0, STRIPS // 2 - 1) as i:
                    for j in range(2):
                        n1 = pool.snap(n0 + i * 2 + (1 + j))
                        ahead = pool.snap(n1 + 1)
                        loads = pool.snap(u0 + i * IN + IN)
                        conv_inputs(ahead, loads, j, 0)
                        attention(n1)
                        conv_inputs(ahead, loads, j, 1, (0, 1))
                        feed_forward(pool.snap(n1 - 1))
                        conv_inputs(ahead, loads, j, 1, (2, 3))
                last = pool.snap(n0 + (STRIPS - 1))
                attention(last)
                feed_forward(pool.snap(last - 1))
                feed_forward(last)

        @block.scalar
        def _(sc):
            def make_gate(pair):
                sc.wait_ge(gate_pe, pair * 3 + 1)
                for a in range(2):
                    last = sc.activation(hidden[:, a:a + 1], scr[a][0:SE, 0:1], ACT.Relu, bias=se1_b[:],
                                         scale=1.0 / (H * W))
                last.then_inc(gate_act, 1)
                sc.wait_ge(gate_pe, pair * 3 + 2)
                sc.activation(gate[:], scr[1][:, 16:18], ACT.Sigmoid, bias=se2_b[:]).then_inc(gate_act, 1)

            def attention(n1, following, s, before=None):
                if following is not None:
                    sc.wait_ge(sum_ok, n1)
                    sc.dma_start(xg[:], x_pair[following, :, bass.ds(s * WS, WS), :].rearrange("c h w -> c (h w)"))\
                        .then_inc(xg_in, 16)
                for j in range(CH):
                    if j == 2 and before:
                        gelu(before[2])
                    sc.wait_ge(g_ps[j], n1)
                    sc.activation(g[:, 8 * j:8 * j + 8].rearrange("c k w -> c (k w)"), proj[j % 2][:],
                                  ACT.Identity, bias=g_b[:]).then_inc(g_sb[j], 1)
                if before:
                    components(*before)
                if following is not None:
                    sc.wait_ge(xg_in, sc.snap(n1 * 16))
                    sc.activation(xg[:], xg[:], ACT.Copy, accum_out=sums[:, bass.ds(s, 1)]).then_inc(sum_ok, 1)
                relu(n1, 0)
                for j in range(CH):
                    sc.wait_ge(s_sub[j], n1)
                    sc.activation(prob[:, j], prob[:, j], ACT.Exp).then_inc(s_exp[j], 1)

            def relu(n1, q):
                sc.wait_ge(c_out[q], n1 + q)
                sc.activation(hid[:, q], cout[:, q].rearrange("c (r w) o -> c r (w o)", r=4), ACT.Relu,
                              bias=conv_b[:]).then_inc(c_sb[q], 1)

            def transposed(n1):
                relu(n1, 1)
                for j in range(CH):
                    sc.wait_ge(t_ps[j], n1)
                    for e in range(2):
                        rows = slice(64 * e, 64 * e + 64)
                        last = sc.activation(probT[rows, j, :, :, rows],
                                             proj[j % 2][rows].rearrange("c (r o w) -> c r o w", r=4, o=2), ACT.Identity)
                    last.then_inc(t_sb[j], 1)

            def token_major(m1):
                m8 = sc.snap((m1 - 1) * (TILES // 2))
                for k in range(TILES // 2):
                    sc.wait_ge(f_ps, m8 + (k + 1))
                    sc.activation(ff[:, 2 * k:2 * k + 2, :], token_banks[k % 4][:].rearrange("c (r w) -> c r w", r=2),
                                  ACT.Identity).then_inc(f_sb, 1)

            def gelu(m1):
                for k in range(2):
                    tl = slice(k * TILES // 2, (k + 1) * TILES // 2)
                    sc.wait_ge(hbias[k], m1)
                    last = sc.activation(act_h[:, tl], act_h[:, tl], ACT.Gelu_apprx_tanh)
                last.then_inc(hact, 1)

            def components(pair, s, m1, m32):
                for r in range(2):
                    sc.wait_ge(z_ps[r], m1)
                    if r == 0:
                        sc.wait_ge(z_out, m32)
                    sc.activation(zs[0:COMP, r, :], acc[r][0:COMP, :], ACT.Identity)
                    sc.activation(zs[64:64 + COMP, r, :], acc[r][64:64 + COMP, :], ACT.Identity).then_inc(z_sb[r], 1)
                sc.wait_ge(z_sb[0], m1 + 1)
                sc.wait_ge(z_sb[1], m1 + 1)
                for part in range(2):
                    sc.dma_start(zv[pair, s, part], zs[64 * part:64 * part + COMP].rearrange(
                        "k g (r c) -> k (g r) c", r=4)).then_inc(z_out, 16)

            sc.sem_inc(z_out, 32)
            sc.sem_inc(z_sb[0], 1)
            sc.sem_inc(z_sb[1], 1)
            sc.sem_inc(sum_ok, 1)

            def strips(pair, following):
                n0 = sc.snap(pair * STRIPS + 1)
                make_gate(pair)
                attention(n0, following, 0)
                transposed(n0)
                second = sc.snap(n0 + 1)
                attention(second, following, 1)
                token_major(n0)
                transposed(second)
                with sc.Fori(0, STRIPS - 2) as s:
                    m1 = sc.snap(n0 + s)
                    n1 = sc.snap(m1 + 2)
                    attention(n1, following, sc.snap(s + 2), (pair, s, m1, sc.snap(m1 * 32)))
                    token_major(sc.snap(m1 + 1))
                    transposed(n1)
                last = sc.snap(n0 + (STRIPS - 1))
                before = sc.snap(last - 1)
                gelu(before)
                components(pair, STRIPS - 2, before, sc.snap(before * 32))
                token_major(last)
                gelu(last)
                components(pair, STRIPS - 1, last, sc.snap(last * 32))

            with sc.Fori(0, PAIRS - 1) as pair:
                strips(pair, sc.snap(pair + 1))
            strips(PAIRS - 1, None)
            sc.wait_ge(z_out, 32 * (PAIRS * STRIPS + 1))

        @block.vector
        def _(v):
            v.memset(zrow[:], 0.0).then_inc(pads, 1)
            for par in range(2):
                v.memset(xs[par][:, :, :, 0:W + 2:W + 1], 0.0)
                v.memset(xs[par][0:C, :, 0, 1:W + 1], 0.0)
                v.memset(xs[par][C:128, :, 5, 1:W + 1], 0.0).then_inc(pads, 1)
            v.memset(xz[:], 0.0)
            v.memset(probT[:], 0.0).then_inc(pads, 1)
            v.wait_ge(pads, 4)

            def values(n1):
                for j in range(CH):
                    v.wait_ge(v_ps[j], n1)
                    v.tensor_tensor(val[:, j], proj[j % 2][:].rearrange("c (r w) -> c r w", r=4),
                                    val_b[:].unsqueeze(1).to_broadcast([128, 4, 128]), ALU.add).then_inc(v_sb[j], 1)

            def softmax(n1):
                for j in range(CH):
                    scores = scr[j % 2][:].rearrange("c (r w) -> c r w", r=8)
                    v.wait_ge(s_ps[j], n1)
                    v.tensor_reduce(mx[:, j], scores, AX_X, ALU.max).then_inc(s_max[j], 1)
                    v.wait_ge(s_max[j], n1)
                    v.tensor_tensor(prob[:, j], scores, mx[:, j].unsqueeze(2).to_broadcast([128, 8, 64]),
                                    ALU.subtract).then_inc(s_sub[j], 1)
                for j in range(CH):
                    v.wait_ge(s_exp[j], n1)
                    v.tensor_reduce(den[:, j], prob[:, j], AX_X, ALU.add).then_inc(s_sum[j], 1)
                    v.wait_ge(s_sum[j], n1)
                    v.reciprocal(rden[:, j], den[:, j]).then_inc(s_rec[j], 1)

            def with_layer_norm(n1, m1, par, following=None):
                statistics(m1)
                residual(n1, par, (0, 1))
                if following:
                    reorder(*following)
                scaled(m1)
                residual(n1, par, (2, 3))

            def statistics(m1):
                m8 = v.snap((m1 - 1) * (TILES // 2))
                for k in range(TILES // 2):
                    v.wait_ge(f_sb, m8 + (k + 1))
                    for tl in (2 * k, 2 * k + 1):
                        for a in range(2):
                            st = v.bn_stats(stats[:, tl, a, :], ff[:, tl, a * C:a * C + C])
                st.then_inc(stat_ok, 1)
                v.wait_ge(stat_ok, m1)
                v.tensor_tensor(dmean[:], stats[:, :, :, 1], stats[:, :, :, 4], ALU.subtract).then_inc(dm_ok, 1)
                v.tensor_tensor(msum[:], stats[:, :, :, 2], stats[:, :, :, 5], ALU.add).then_inc(dm_ok, 1)
                v.wait_ge(dm_ok, m1 + m1)
                v.scalar_tensor_tensor(out=dsq[:], in0=dmean[:], scalar=0.25, in1=dmean[:], op0=ALU.mult,
                                       op1=ALU.mult).then_inc(q_ok, 1)
                v.tensor_scalar(msum[:], msum[:], 1.0 / C, LN_EPS, ALU.mult, ALU.add).then_inc(ve_ok, 1)
                v.wait_ge(q_ok, m1)
                v.wait_ge(ve_ok, m1)
                v.tensor_tensor(vare[:], dsq[:], msum[:], ALU.add).then_inc(var_ok, 1)

            def scaled(m1):
                v.wait_ge(rstd_ok, m1)
                v.tensor_tensor(act_h[:].rearrange("p t (a c) -> p (t a) c", a=2),
                                ff[:, :, 128:256].rearrange("p t (a c) -> p t a c", a=2),
                                rstd[:].unsqueeze(3).to_broadcast([128, TILES, 2, C]), ALU.mult).then_inc(hmul, 1)

            def biased(m1):
                v.wait_ge(hmul, m1)
                for k in range(2):
                    tl = slice(k * TILES // 2, (k + 1) * TILES // 2)
                    v.tensor_tensor(act_h[:, tl], act_h[:, tl],
                                    ffn_b[:].unsqueeze(1).to_broadcast([128, TILES // 2, 128]), ALU.add)\
                        .then_inc(hbias[k], 1)

            def residual(n1, par, chunks):
                for j in chunks:
                    v.wait_ge(a_ps[j], n1)
                    at = slice(64 * j, 64 * j + 64)
                    v.tensor_tensor(x1[:, :, at], acc[j % 2][:].rearrange("c (h w) -> c h w", h=WS),
                                    xt[par][:, :, at], ALU.add).then_inc(x1_sb[j], 1)

            def windows(rows, par, j):
                return xt[par][rows, :, 64 * j:64 * j + 64].rearrange("c h (k w) -> c k h w", w=WS)

            def reorder(loads, par):
                v.wait_ge(x_in[par], loads)
                for j in range(CH):
                    v.tensor_copy(xw[:, 8 * j:8 * j + 8].rearrange("c k (h w) -> c k h w", w=WS),
                                  windows(slice(0, 128), par, j)).then_inc(xw_sb[j], 1)

            def separate(par):
                for j in range(CH):
                    for a in range(2):
                        rows = slice(a * C, a * C + C)
                        last = v.tensor_copy(xz[rows, 8 * j:8 * j + 8, a].rearrange("c k (h w) -> c k h w", w=WS),
                                             windows(rows, par, j))
                    last.then_inc(xz_sb[j], 1)

            def attention(n1, par, pair=None, scaled_before=None):
                conv_outputs(n1, 0)
                if scaled_before is not None:
                    biased(scaled_before)
                separate(par)
                if pair is not None:
                    value_weights(pair)
                values(n1)
                softmax(n1)
                conv_outputs(n1, 1)

            def conv_outputs(n1, q):
                m = [wide[k // 2][:, k % 2 * 256:k % 2 * 256 + 256] for k in range(4)]
                v.wait_ge(c_ps[q], n1 + 1)
                v.tensor_copy(msum12[:, q], m[1]).then_inc(c_half[q], 1)
                v.wait_ge(c_half[q], n1 * 3 - 2)
                v.tensor_tensor(mdif12[:, q], msum12[:, q], m[2], ALU.subtract)
                v.tensor_tensor(msum12[:, q], msum12[:, q], m[2], ALU.add).then_inc(c_half[q], 2)
                v.wait_ge(c_half[q], n1 * 3)
                v.tensor_tensor(cout[:, q, :, 0], msum12[:, q], m[0], ALU.add)
                v.tensor_tensor(cout[:, q, :, 1], mdif12[:, q], m[3], ALU.subtract).then_inc(c_out[q], 1)

            def value_weights(pair):
                v.wait_ge(gate_act, pair * 2 + 2)
                v.tensor_copy(gate_wide[:], gate[0:C].unsqueeze(2).to_broadcast([C, 2, 128])).then_inc(gate_dve, 1)
                v.wait_ge(gate_pe, pair * 3 + 3)
                v.tensor_copy(gate_row[:], scr[0][:, 0:128].rearrange("q (a c) -> q a c", a=2)).then_inc(gate_dve, 1)
                v.wait_ge(gate_dve, pair * 4 + 3)
                for a in range(2):
                    s = slice(a * C, a * C + C)
                    v.tensor_tensor(val_w[s, s], gate_row[s, a], vw_plain[s, :], ALU.mult)
                    last = v.tensor_tensor(val_b[:, s], gate_row[:, a], obv_row[:], ALU.mult)
                last.then_inc(gate_dve, 1)
                v.wait_ge(gate_dve, pair * 4 + 4)
                for a in range(2):
                    s = slice(a * C, a * C + C)
                    last = v.tensor_tensor(val_b[:, s], val_b[:, s], ms2b_row[:], ALU.add)
                last.then_inc(pair_w, 1)
                v.wait_ge(pair_w, pair + 1)

            v.sem_inc(c_out[1], 1)
            for j in range(CH):
                v.sem_inc(x1_sb[j], 2)
            with v.Fori(0, PAIRS) as pair:
                n0 = v.snap(pair * STRIPS + 1)
                u0 = v.snap(pair * (IN * STRIPS // 2) + IN)
                v.wait_ge(sum_ok, n0)
                v.tensor_reduce(gap[:], sums[:], AX_X, ALU.add).then_inc(gate_dve, 1)
                reorder(u0, 0)
                attention(n0, 0, pair)
                residual(n0, 0, range(CH))
                reorder(u0, 1)
                second = v.snap(n0 + 1)
                attention(second, 1)
                with_layer_norm(second, n0, 1, (v.snap(u0 + IN), 0))
                with v.Fori(0, STRIPS // 2 - 2) as i:
                    for j in range(2):
                        m1 = v.snap(n0 + i * 2 + j)
                        n1 = v.snap(m1 + 2)
                        attention(n1, j, scaled_before=m1)
                        with_layer_norm(n1, v.snap(m1 + 1), j, (v.snap(u0 + i * IN + IN * (1 + j)), 1 - j))
                last = v.snap(n0 + (STRIPS - 1))
                before = v.snap(last - 1)
                attention(before, 0, scaled_before=v.snap(before - 2))
                with_layer_norm(before, v.snap(before - 1), 0, (v.snap(u0 + IN * (STRIPS // 2 - 1)), 1))
                attention(last, 1, scaled_before=v.snap(last - 2))
                with_layer_norm(last, before, 1)
                biased(before)
                statistics(last)
                scaled(last)
                biased(last)

        @block.tensor
        def _(p):
            def mm(o, l, r, start=True, stop=True):
                return p.matmul(o, l, r, start=start, stop=stop, skip_group_check=True)

            def project_scores(n1, chunks):
                for j in chunks:
                    if j >= 2:
                        p.wait_ge(g_sb[j - 2], n1)
                    p.wait_ge(xw_sb[j], n1)
                    mm(proj[j % 2][:], g_w[:], xw[:, 8 * j:8 * j + 8].rearrange("c k w -> c (k w)"))\
                        .then_inc(g_ps[j], 1)

            def project_values(n1):
                for j in range(CH):
                    if j < 2:
                        p.wait_ge(g_sb[j + 2], n1)
                    else:
                        p.wait_ge(v_sb[j - 2], n1)
                    p.sem_inc(waited, 1)
                    for m in range(2):
                        for odd in range(2):
                            for up in range(2):
                                k = 2 * m + odd
                                last = mm(proj[j % 2][64 * up:64 * up + 64, 128 * k:128 * k + 128],
                                          xw[:, 8 * j + 4 * m + 2 * up + odd], val_w[:])
                    last.then_inc(v_ps[j], 1)

            def convolve(n1, q, products=(0, 1, 2, 3)):
                if products[0] == 0:
                    p.wait_ge(c_in[q], n1)
                    p.wait_ge(c_out[1 - q], n1)
                for k in products:
                    for pr in range(2):
                        for odd in range(2):
                            for a in range(2):
                                r = odd + pr
                                o = 64 * odd + 32 * a
                                last = mm(wide[k // 2][o:o + HID, k % 2 * 256:k % 2 * 256 + 256],
                                          conv_w[:, odd, pr, k, :], cin[:, q, k, a, r:r + 4, :],
                                          pr == 0 and k % 2 == 0, pr == 1)
                if products[-1] == 3:
                    last.then_inc(c_ps[q], 1)

            def scores(n1, chunks):
                for j in chunks:
                    p.wait_ge(g_sb[j], n1)
                    p.wait_ge(xz_sb[j], n1)
                    if j >= 2:
                        p.wait_ge(s_sub[j - 2], n1)
                    p.sem_inc(waited, 1)
                    for k in range(4):
                        for odd in range(2):
                            w = 8 * j + 2 * k + odd
                            last = mm(scr[j % 2][64 * odd:64 * odd + 64].rearrange(
                                "q (a k s) -> q a k s", a=2, k=4)[:, :, k, :], g[:, w], xz[:, w])
                    last.then_inc(s_ps[j], 1)

            def transpose(n1, chunks, m1=None):
                for j in chunks:
                    p.wait_ge(s_nrm[j], n1)
                    if j < 2 and m1 is None:
                        p.wait_ge(v_sb[j + 2], n1)
                    elif j < 2:
                        p.wait_ge(f_sb, (m1 - 1) * (TILES // 2) + (5 + j))
                    else:
                        p.wait_ge(t_sb[j - 2], n1)
                    for k in range(4):
                        last = p.transpose(proj[j % 2][:, 128 * k:128 * k + 128],
                                           prob[:, j, 2 * k:2 * k + 2, :].rearrange("c k s -> c (k s)"), ident[:])
                    last.then_inc(t_ps[j], 1)

            def convolved(n1, chunks, z1=None):
                for j in chunks:
                    if j % 2 == 0:
                        p.wait_ge(c_sb[j // 2], n1)
                    if j < 2 and z1 is not None:
                        p.wait_ge(z_sb[j], z1)
                    if j >= 2:
                        p.wait_ge(x1_sb[j - 2], n1 + 2)
                    bank = acc[j % 2][:].rearrange("c (h w) -> c h w", h=WS)
                    for par in range(2):
                        mm(bank[:, par:WS:2], ms2_w[:, par, :], hid[:, j // 2, :, 64 * (j % 2):64 * (j % 2) + 64],
                           par == 0, False)

            def attended(n1, chunks):
                for j in chunks:
                    p.wait_ge(t_sb[j], n1)
                    p.sem_inc(waited, 1)
                    for m in range(2):
                        for odd in range(2):
                            for a in range(2):
                                c = slice(a * C, a * C + C)
                                o = acc[j % 2][c].rearrange("c (h m u o w) -> c m o u h w", h=WS, m=2, u=2, o=2)
                                last = mm(o[:, m, odd], val[:, j, 2 * m + odd, c], probT[:, j, 2 * a + m, odd, :],
                                          False, m == 1 and odd == 1)
                    last.then_inc(a_ps[j], 1)

            def token_major(m1, n1):
                m8 = p.snap((m1 - 1) * (TILES // 2))
                for k in range(TILES // 2):
                    if k == 0:
                        for j in range(CH):
                            p.wait_ge(x1_sb[j], m1 + 2)
                    if k < 2:
                        p.wait_ge(v_sb[k + 2], n1)
                    elif k < 4:
                        p.wait_ge(s_sub[k], n1)
                    else:
                        p.wait_ge(f_sb, m8 + (k - 3))
                    for e in range(2):
                        p.transpose(token_banks[k % 4][:, 256 * e:256 * e + 128], x1[:, k, e * HALF:e * HALF + HALF], ident[:])
                    for e in range(2):
                        for up in range(2):
                            q = slice(64 * up, 64 * up + 64)
                            last = mm(token_banks[k % 4][q, 256 * e + 128:256 * e + 256],
                                      x1[:, k, e * HALF + 64 * up:e * HALF + 64 * up + 64], ffn_w[:])
                    last.then_inc(f_ps, 1)

            def components(m1, x1):
                p.wait_ge(hact, m1)
                for r in range(2):
                    p.wait_ge(x1_sb[2 + r], x1)
                    for e in range(2):
                        tl = slice(8 * r + e, 8 * r + 8, 2)
                        mm(acc[r][0:COMP, :], colb[:, e, :], ff[:, tl, 0:128], e == 0, e == 1)
                        last = mm(acc[r][64:64 + COMP, :], colb[:, e, :], act_h[:, tl, :], e == 0, e == 1)
                    last.then_inc(z_ps[r], 1)

            def squeeze(pair):
                p.wait_ge(gate_dve, pair * 4 + 1)
                p.sem_inc(waited, 1)
                for a in range(2):
                    s = slice(a * C, a * C + C)
                    last = mm(scr[a][0:SE, 0:1], se1_t[s, :], gap[s, :])
                last.then_inc(gate_pe, 1)

            def excite(pair):
                p.wait_ge(gate_act, pair * 2 + 1)
                p.sem_inc(waited, 1)
                mm(scr[1][:, 16:18], se2_t[:].rearrange("o a c -> o (a c)"), hidden[:]).then_inc(gate_pe, 1)

            def spread(pair):
                p.wait_ge(gate_dve, pair * 4 + 2)
                p.sem_inc(waited, 1)
                for a in range(2):
                    last = mm(scr[0][:, a * C:a * C + C], gate_wide[:, a, :], ident[0:C, 0:C])
                last.then_inc(gate_pe, 1)

            def attention(n1, m1=None, pair=None):
                if pair is not None:
                    squeeze(pair)
                if pair is None:
                    convolve(n1, 0)
                else:
                    convolve(n1, 0, (0, 1))
                    excite(pair)
                    convolve(n1, 0, (2, 3))
                project_scores(n1, (0, 1))
                project_scores(n1, (2, 3))
                if pair is not None:
                    spread(pair)
                convolve(n1, 1, (0, 1))
                if m1 is not None:
                    components(m1, n1 + 1)
                if pair is not None:
                    p.wait_ge(pair_w, pair + 1)
                project_values(n1)
                scores(n1, (0, 1))
                convolve(n1, 1, (2,))
                scores(n1, (2, 3))
                convolve(n1, 1, (3,))

            def finish(n1, z1=None, m1=None):
                transpose(n1, (0, 1), m1)
                convolved(n1, (0, 1), z1)
                transpose(n1, (2, 3))
                attended(n1, (0, 1))
                for j in (2, 3):
                    convolved(n1, (j,))
                    attended(n1, (j,))

            for q in range(2):
                p.sem_inc(c_ps[q], 1)
            p.wait_ge(consts_in, 16)
            p.wait_ge(pads, 4)
            with p.Fori(0, PAIRS) as pair:
                n0 = p.snap(pair * STRIPS + 1)
                attention(n0, pair=pair)
                finish(n0, n0)
                second = p.snap(n0 + 1)
                attention(second)
                token_major(n0, second)
                finish(second, m1=n0)
                with p.Fori(0, STRIPS // 2 - 1) as i:
                    for j in range(2):
                        m1 = p.snap(n0 + i * 2 + j)
                        n1 = p.snap(m1 + 2)
                        attention(n1, m1)
                        before = p.snap(m1 + 1)
                        token_major(before, n1)
                        finish(n1, before, before)
                last = p.snap(n0 + (STRIPS - 1))
                components(p.snap(last - 1), last + 2)
                token_major(last, last)
                p.wait_ge(z_sb[0], last)
                p.wait_ge(z_sb[1], last)
                components(last, last + 2)


def modes_and_output(nc, t, comps, out, keep):
    with ExitStack() as ctx:
        def sb(name, shape):
            return ctx.enter_context(nc.sbuf_tensor(name, shape, F32))

        RING = 5
        QK = 4
        BLURRED = 2 * RADIUS + B
        banks = [ctx.enter_context(nc.psum_tensor(f"tb{i}", [128, BANK], F32)) for i in range(8)]
        work = sb("work", [128, RING * 2 * QK * 256])
        mixed = work[0:C, 0:BLURRED * MM].rearrange("c (b m) -> c b m", b=BLURRED)
        yblur = work[0:C, BLURRED * MM:(BLURRED + B) * MM].rearrange("c (b m) -> c b m", b=B)

        with ExitStack() as c1:
            xx = c1.enter_context(nc.sbuf_tensor("xx", [128, M, M, B], F32))
            w = c1.enter_context(nc.sbuf_tensor("w", [128, C, M, M], F32))
            w_in = c1.enter_context(nc.semaphore("w_in"))
            transform_rows(nc, t, comps, keep, banks, work, xx, w, w_in)
            mix_modes(nc, keep, banks, mixed, yblur, xx, w, w_in)
        invert(nc, t, out, banks, yblur)


def transform_rows(nc, t, comps, keep, banks, work, xx, w, w_in):
    with ExitStack() as ctx:
        def sb(name, shape):
            return ctx.enter_context(nc.sbuf_tensor(name, shape, F32))

        def sem(name):
            return ctx.enter_context(nc.semaphore(name))

        fc2_w, same_w, ident = keep["fc2_w"], keep["same_w"], keep["ident"]
        QK, GROUPS = 4, M // 4
        LOADS = 2 * GROUPS
        RING = GROUPS
        ring = work[:].rearrange("h (u s c) -> h u s c", u=RING, s=2)
        rowb = sb("rowb", [128, 2, M, 2, 32])
        drow = sb("drow", [128, GROUPS, 256])
        dsb = sb("dsb", [128, 2, MM])
        consts = sem("tail_consts")
        loaded = [sem(f"loaded{i}") for i in range(RING)]
        used = [sem(f"used{i}") for i in range(RING)]
        d_sb, t_ps, t_sb, u_ps, u_sb = (sem(n) for n in ("d_sb", "dt_ps", "dt_sb", "u_ps", "u_sb"))
        block = ctx.enter_context(nc.Block())

        cv = comps.rearrange("p (f h) (s g q) m c -> p f h g s (q m c)", f=2, s=2, q=QK)

        @block.sync
        def _(sp):
            sp.dma_start(rowb[:].rearrange("p a b c d -> p (a b c d)"), t["k_rowb"]).then_inc(consts, 16)
            with sp.Fori(0, PAIRS) as pair:
                for u in range(LOADS):
                    sp.wait_ge(used[u % RING], pair * 2 + (u // RING + 1))
                    sp.dma_start(ring[:, u % RING], cv[pair, u // GROUPS, :, u % GROUPS]).then_inc(loaded[u % RING], 16)

        @block.scalar
        def _(sc):
            sc.wait_ge(used[RING - 1], 3)
            for lo in (0, C):
                sc.dma_start(w[lo:lo + C], t["w1"]).then_inc(w_in, 16)

        @block.tensor
        def _(p):
            for u in range(RING):
                p.sem_inc(used[u], 1)
            p.wait_ge(consts, 16)
            with p.Fori(0, PAIRS) as pair:
                n1 = p.snap(pair + 1)
                p.wait_ge(d_sb, n1)
                for u in range(LOADS):
                    half, g = u // GROUPS, u % GROUPS
                    p.wait_ge(loaded[u % RING], (pair * 2 + (u // RING + 1)) * 16)
                    for cs in range(2):
                        for q in range(QK):
                            last = p.matmul(banks[g // 2][32 * q:32 * q + 32, g % 2 * 256:g % 2 * 256 + 256],
                                            rowb[:, half, QK * g + q, cs, :], ring[:, u % RING, cs, 256 * q:256 * q + 256],
                                            start=half == 0 and cs == 0 and g % 2 == 0, stop=half == 1 and cs == 1,
                                            skip_group_check=True)
                    last.then_inc(used[u % RING], 1)
                p.wait_ge(d_sb, n1 + 1)
                for g in range(GROUPS):
                    for part in range(2):
                        dst = banks[3 + part][:, 128 * g:128 * g + 128] if g < 4 else \
                            banks[5][:, 128 * part:128 * part + 128]
                        last = p.transpose(dst, drow[:, g, 128 * part:128 * part + 128], ident[:])
                last.then_inc(t_ps, 1)
                p.wait_ge(t_sb, n1)
                p.wait_ge(u_sb, n1)
                for a in range(2):
                    p.matmul(banks[6 + a][:, 0:MM], fc2_w[:, a, :], dsb[:, 1, :], start=True, stop=False,
                             skip_group_check=True)
                    last = p.matmul(banks[6 + a][:, 0:MM], same_w[:, a, :], dsb[:, 0, :], start=False, stop=True,
                                    skip_group_check=True)
                last.then_inc(u_ps, 1)

        @block.vector
        def _(v):
            v.sem_inc(d_sb, 1)
            v.sem_inc(u_sb, 1)
            with v.Fori(0, PAIRS) as pair:
                n1 = v.snap(pair + 1)
                for g in range(0, GROUPS, 2):
                    n = min(2, GROUPS - g)
                    for h in range(n):
                        v.wait_ge(used[g + h], pair * 2 + 3)
                    last = v.tensor_copy(drow[:, g:g + n, :].rearrange("q g c -> q (g c)"), banks[g // 2][:, 0:256 * n])
                last.then_inc(d_sb, 1)
                v.wait_ge(t_ps, n1)
                for part in range(2):
                    v.tensor_copy(dsb[:, part].rearrange("c (k n) -> c n k", n=M)[:, 0:16],
                                  banks[3 + part][:].rearrange("c (n k) -> c n k", k=32)[:, :, 0:M])
                v.tensor_copy(dsb[:].rearrange("c m (k n) -> c m n k", n=M)[:, :, 16:M],
                              banks[5][:, 0:256].rearrange("c (m n k) -> c m n k", m=2, k=32)[:, :, :, 0:M])\
                    .then_inc(t_sb, 1)
                v.wait_ge(u_ps, n1)
                for a in range(2):
                    at = v.snap(pair * 2 + a)
                    src = banks[6 + a][:, 0:MM].rearrange("c (i j) -> c i j", i=M)
                    dst = xx[:, :, :, bass.ds(at, 1)].rearrange("c i j o -> c i (j o)")
                    v.tensor_copy(dst[0:C], src[0:C])
                    for di, si in ((slice(0, 1), slice(0, 1)), (slice(1, M), slice(M - 1, 0, -1))):
                        for dj, sj in ((slice(0, 1), slice(0, 1)), (slice(1, M), slice(M - 1, 0, -1))):
                            last = v.tensor_copy(dst[C:128, di, dj], src[C:128, si, sj])
                last.then_inc(u_sb, 1)


def mix_modes(nc, keep, banks, mixed, yblur, xx, w, w_in):
    with ExitStack() as ctx:
        def sb(name, shape):
            return ctx.enter_context(nc.sbuf_tensor(name, shape, F32))

        def sem(name):
            return ctx.enter_context(nc.semaphore(name))

        fc2_b = keep["fc2_b"]
        DEEP = 4
        wm = [sb(f"wm{i}", [128, C, M]) for i in range(DEEP)]
        sign = sb("sign", [128, 1])
        w_ok, m_ps, m_sb = sem("w_ok"), sem("m_ps"), sem("m_sb")
        setup, bias_ok, blur_pass = sem("setup"), sem("bias_ok"), sem("blur_pass")
        BR = 5
        taps = blur_taps()
        block = ctx.enter_context(nc.Block())

        @block.scalar
        def _(sc):
            mp = mixed.rearrange("c b (i j) -> c b i j", i=M)
            for i in range(M):
                sc.wait_ge(m_ps, i + 1)
                for odd in range(2):
                    src = banks[i % 4][C * odd:C * odd + C, 0:M // 2 * B].rearrange("c (j b) -> c b j", b=B)
                    dst = mp[:, :, i, odd:M:2]
                    sc.activation(dst[:, RADIUS:RADIUS + B], src, ACT.Identity)
                    for lo, image in ((0, 0), (RADIUS + B, B - 1)):
                        last = sc.activation(dst[:, lo:lo + RADIUS],
                                             src[:, image:image + 1].to_broadcast([C, RADIUS, M // 2]), ACT.Identity)
                last.then_inc(m_sb, 1)

        @block.vector
        def _(v):
            v.memset(sign[0:C], 1.0)
            v.memset(sign[C:128], -1.0).then_inc(setup, 1)
            v.wait_ge(setup, 1)
            v.tensor_scalar(xx[:, 0, 0, :], xx[:, 0, 0, :], fc2_b[:], None, ALU.add).then_inc(bias_ok, 1)
            passes = [0]

            def blur(block_of_rows):
                at = slice(block_of_rows * BR * M, (block_of_rows + 1) * BR * M)
                v.wait_ge(m_sb, (block_of_rows + 1) * BR)
                for k in range(2 * RADIUS + 1):
                    if k == 0:
                        last = v.tensor_scalar(yblur[:, :, at], mixed[:, 0:B, at], float(taps[0]), None, ALU.mult)
                    else:
                        v.wait_ge(blur_pass, passes[0])
                        last = v.scalar_tensor_tensor(out=yblur[:, :, at], in0=mixed[:, k:k + B, at],
                                                      scalar=float(taps[k]), in1=yblur[:, :, at],
                                                      op0=ALU.mult, op1=ALU.add)
                    last.then_inc(blur_pass, 1)
                    passes[0] += 1

            v.wait_ge(w_in, 32)
            for i in range(M):
                k, neg = i % DEEP, (M - i) % M
                if i >= DEEP:
                    v.wait_ge(m_ps, i - DEEP + 1)
                v.scalar_tensor_tensor(out=wm[k][:, :, 0:1], in0=w[:, :, neg, 0:1], scalar=sign[:],
                                       in1=w[:, :, i, 0:1], op0=ALU.mult, op1=ALU.add)
                v.scalar_tensor_tensor(out=wm[k][:, :, 1:M], in0=w[:, :, neg, M - 1:0:-1], scalar=sign[:],
                                       in1=w[:, :, i, 1:M], op0=ALU.mult, op1=ALU.add).then_inc(w_ok, 1)
                if i > BR and i % BR == 1:
                    blur(i // BR - 1)
            blur(M // BR - 1)

        @block.tensor
        def _(p):
            p.wait_ge(bias_ok, 1)
            for i in range(M):
                p.wait_ge(w_ok, i + 1)
                if i >= 4:
                    p.wait_ge(m_sb, i - 3)
                for j in range(M):
                    last = p.matmul(banks[i % 4][C * (j % 2):C * (j % 2) + C, j // 2 * B:j // 2 * B + B],
                                    wm[i % DEEP][:, :, j], xx[:, i, j, :], start=True, stop=True)
                last.then_inc(m_ps, 1)


def invert(nc, t, out, banks, yblur):
    with ExitStack() as ctx:
        def sb(name, shape):
            return ctx.enter_context(nc.sbuf_tensor(name, shape, F32))

        def sem(name):
            return ctx.enter_context(nc.semaphore(name))

        def sems(name, n):
            return [sem(f"{name}{i}") for i in range(n)]

        GO = 4
        GROUPS = C // GO
        DEEP = 4
        P2 = M + 2
        ycur = sb("ycur", [128, P2, P2])
        blurc = sb("blurc", [128, C])
        inv = sb("inv", [128, 2, H])
        invc = sb("invc", [128, 2, KEPT])
        tcur = sb("tcur", [128, 32, C])
        rr = [sb(f"rr{i}", [128, 2 * KEPT]) for i in range(2)]
        stage = [[sb(f"stage{i}_{hh}", [128, GO, W]) for hh in range(2)] for i in range(DEEP)]
        tail_in, clear = sem("tail_in"), sem("clear")
        y_sb, t_ps, t_sb = sem("y_sb"), sem("t_ps"), sem("t_sb")
        r_ps, r_sb = sem("r_ps"), sem("r_sb")
        o_ps = sems("o_ps", 2)
        o_sb = sems("o_sb", 2)
        stored = [sems(f"stored{hh}_", DEEP) for hh in range(2)]
        block = ctx.enter_context(nc.Block())

        def evacuate(eng, copy, b, n16, g, hh):
            slot = g % DEEP
            eng.wait_ge(o_ps[hh], n16 + g)
            eng.wait_ge(stored[hh][slot], (b * (GROUPS // DEEP) + (g // DEEP + 1)) * 16)
            for oo in range(2):
                src = banks[4 + 2 * hh + oo][:, 0:2 * KEPT].rearrange("h (o w) -> h o w", w=KEPT)
                copy(stage[slot][hh][:, oo:GO:2, 0:KEPT_LO], src[:, :, 0:KEPT_LO])
                last = copy(stage[slot][hh][:, oo:GO:2, W - KEPT_HI:W], src[:, :, KEPT_LO:KEPT])
            last.then_inc(o_sb[hh], 1)

        @block.sync
        def _(sp):
            for dst, src in ((blurc[:], t["k_blurc"]), (inv[:], t["k_inv"]), (invc[:], t["k_invc"])):
                sp.dma_start(dst, src).then_inc(tail_in, 16)
            with sp.Fori(0, B) as b:
                n16 = sp.snap(b * GROUPS + 2)
                for g in range(GROUPS):
                    for hh in range(2):
                        sp.wait_ge(o_sb[hh], n16 + g)
                        sp.dma_start(out[b, g * GO:g * GO + GO, hh * 128:hh * 128 + 128, :]
                                     .rearrange("o h w -> h o w"), stage[g % DEEP][hh][:])\
                            .then_inc(stored[hh][g % DEEP], 16)
            for hh in range(2):
                for slot in range(DEEP):
                    sp.wait_ge(stored[hh][slot], 16 * (B * GROUPS // DEEP + 1))

        @block.gpsimd
        def _(pool):
            for slot in range(DEEP):
                pool.memset(stage[slot][0][:, :, KEPT_LO:W - KEPT_HI], 0.0)
            pool.memset(stage[0][1][:, :, KEPT_LO:W - KEPT_HI], 0.0).then_inc(clear, 1)

        @block.vector
        def _(v):
            def first_modes(b):
                v.tensor_copy(ycur[0:C, 1:M + 1, 1:M + 1], yblur[:, bass.ds(b, 1)].rearrange(
                    "c o (i j) -> c (o i) j", i=M)).then_inc(y_sb, 1)

            def transformed(b3, c):
                v.wait_ge(t_ps, b3 + c)
                for q in (0, 32):
                    last = v.tensor_copy(tcur[q:q + M1, 7 * c:7 * c + 7, :],
                                         banks[c % 2][q:q + M1, 0:7 * C].rearrange("q (m o) -> q m o", o=C))
                last.then_inc(t_sb, 1)

            def image(b, more):
                n16 = v.snap(b * GROUPS + 1)
                if more:
                    first_modes(v.snap(b + 1))
                for g in range(GROUPS):
                    if more and g == GROUPS - 2:
                        b3 = v.snap(b * 3 + 4)
                        transformed(b3, 0)
                        transformed(b3, 1)
                    if more and g == GROUPS - 1:
                        transformed(b3, 2)
                    evacuate(v, v.tensor_copy, b, n16, g, 1)

            v.memset(ycur[:], 0.0)
            v.memset(tcur[:], 0.0)
            for slot in range(1, DEEP):
                last = v.memset(stage[slot][1][:, :, KEPT_LO:W - KEPT_HI], 0.0)
            last.then_inc(clear, 1)
            v.sem_inc(o_sb[1], 1)
            for slot in range(DEEP):
                v.sem_inc(stored[1][slot], 16)
            v.wait_ge(clear, 2)
            v.tensor_copy(ycur[0:C, 1:M + 1, 1:M + 1], yblur[:, 0].rearrange("c (i j) -> c i j", i=M)).then_inc(y_sb, 1)
            for c in range(3):
                transformed(1, c)
            with v.Fori(0, B - 1) as b:
                image(b, True)
            image(B - 1, False)

        @block.scalar
        def _(sc):
            def copy(dst, src):
                return sc.activation(dst, src, ACT.Identity)

            sc.sem_inc(o_sb[0], 1)
            for slot in range(DEEP):
                sc.sem_inc(stored[0][slot], 16)
            sc.wait_ge(clear, 2)
            with sc.Fori(0, B) as b:
                n16 = sc.snap(b * GROUPS + 1)
                for g in range(GROUPS + 1):
                    if g < GROUPS:
                        sc.wait_ge(r_ps, n16 + g)
                        copy(rr[g % 2][:], banks[2 + g % 2][:, 0:2 * KEPT]).then_inc(r_sb, 1)
                    if g >= 1:
                        evacuate(sc, copy, b, n16, g - 1, 0)

        @block.tensor
        def _(p):
            def modes(c):
                for m in range(7 * c, 7 * c + 7):
                    for q, y in ((0, ycur[:, m + 1, 1:1 + M1]), (32, ycur[:, m, 0:M1])):
                        last = p.matmul(banks[c % 2][q:q + M1, (m - 7 * c) * C:(m - 7 * c) * C + C], y,
                                        blurc[:], start=True, stop=True)
                last.then_inc(t_ps, 1)

            def columns(g):
                for c in range(2):
                    for oo in range(2):
                        for cs in range(2):
                            q = 64 * oo + 32 * cs
                            last = p.matmul(banks[2 + g % 2][q:q + 32, c * KEPT:c * KEPT + KEPT],
                                            tcur[:, :, g * GO + 2 * c + oo], invc[:, cs, :],
                                            start=True, stop=True, tile_position=(0, q))
                last.then_inc(r_ps, 1)

            def rows(n16, k):
                p.wait_ge(r_sb, n16 + k)
                for hh in range(2):
                    p.wait_ge(o_sb[hh], n16 + k)
                    for oo in range(2):
                        last = p.matmul(banks[4 + 2 * hh + oo][:, 0:2 * KEPT],
                                        inv[:, oo, hh * 128:hh * 128 + 128], rr[k % 2][:], start=True, stop=True)
                    last.then_inc(o_ps[hh], 1)

            def image(b, more):
                n16 = p.snap(b * GROUPS + 1)
                p.wait_ge(t_sb, b * 3 + 3)
                for g in range(GROUPS):
                    columns(g)
                    if more and g == GROUPS - 1:
                        p.wait_ge(y_sb, b + 2)
                        modes(0)
                        modes(1)
                    if g >= 1:
                        rows(n16, g - 1)
                if more:
                    p.wait_ge(t_sb, b * 3 + 4)
                    modes(2)
                rows(n16, GROUPS - 1)

            p.wait_ge(tail_in, 48)
            p.wait_ge(clear, 2)
            p.wait_ge(y_sb, 1)
            modes(0)
            modes(1)
            p.wait_ge(t_sb, 1)
            modes(2)
            with p.Fori(0, B - 1) as b:
                image(b, True)
            image(B - 1, False)


_LAYER0 = ["qk_w", "qk_b", "v_w", "v_b", "out_w", "out_b", "ms1_w", "ms1_b", "ms2_w", "ms2_b", "se1_w", "se1_b",
           "se2_w", "se2_b", "ln_g", "ln_b", "fc1_w", "fc1_b", "fc2_w", "fc2_b"]


def kernel(**inputs):
    import concourse.bacc as _bacc
    from concourse.bass_utils import run_bass_kernel_spmd as _run

    nc = _bacc.Bacc("TRN2", target_bir_lowering=False, num_devices=1)
    arrays, tensors = {}, {}
    given = {"x": inputs["x"], "w1": inputs["L1_conv_w1"]}
    given.update({name: inputs["L0_conv_" + name] for name in _LAYER0})
    tables = {name: a.astype(np.float32) for name, a in shape_constants().items()}
    for name, a in list(given.items()) + list(tables.items()):
        a = np.ascontiguousarray(a)
        arrays[f"in_{name}"] = a
        tensors[name] = nc.dram_tensor(f"in_{name}", a.shape, F32, kind="ExternalInput").ap()
    out = nc.dram_tensor("out_0", (B, C, H, W), F32, kind="ExternalOutput").ap()
    conv_layer_then_hartley_kernel(nc, tensors, out)
    r = _run(nc, [arrays], core_ids=[0])
    return r.results[0]["out_0"]
```
